# Optimizing a Trainium2 kernel written in Bass

```python
import numpy as np
import jax
import jax.numpy as jnp

def _softmax(x, axis=-1):
    return jax.nn.softmax(x, axis=axis)

def _gelu(x):
    return jax.nn.gelu(x, approximate=True)

def _silu(x):
    return jax.nn.silu(x)

def _sigmoid(x):
    return jax.nn.sigmoid(x)

def _layernorm(x, axis=-1, eps=1e-05):
    m = jnp.mean(x, axis=axis, keepdims=True)
    v = jnp.var(x, axis=axis, keepdims=True)
    return (x - m) / jnp.sqrt(v + eps)

def _scatter_add(tgt, idx, src, axis=0):
    return tgt.at[idx].add(src)

def _segment_sum(src, seg, n):
    return jax.ops.segment_sum(src, seg, n)
kernel_name = 'mk_prb_d1_jaxref_r8_142960'

def setup_inputs(seed: int=0):
    np.random.seed(seed)
    _w = jnp.asarray

    def _L0_attn_setup():
        import jax, jax.numpy as jnp
        import numpy as np
        D_MODEL = 128
        LN_EPS = 1e-05
        DEN_EPS = 1e-06

        def _layer_norm(x, g, b):
            mu = jnp.mean(x, axis=-1, keepdims=True)
            var = jnp.mean(jnp.square(x - mu), axis=-1, keepdims=True)
            return (x - mu) * jax.lax.rsqrt(var + LN_EPS) * g + b
        key = jax.random.key(seed)
        ks = jax.random.split(key, 7)
        s = 1.0 / np.sqrt(D_MODEL)
        x = jax.random.normal(ks[0], (4, 256, D_MODEL), dtype=jnp.float32)
        qkv_w = jax.random.uniform(ks[1], (D_MODEL, 3 * D_MODEL), jnp.float32, -s, s)
        qkv_b = jax.random.uniform(ks[2], (3 * D_MODEL,), jnp.float32, -s, s)
        gate_w = jax.random.uniform(ks[3], (D_MODEL, D_MODEL), jnp.float32, -s, s)
        gate_b = jax.random.uniform(ks[4], (D_MODEL,), jnp.float32, -s, s)
        ln_g = jnp.ones((D_MODEL,), jnp.float32)
        ln_b = jnp.zeros((D_MODEL,), jnp.float32)
        return {'x': x, 'qkv_w': qkv_w, 'qkv_b': qkv_b, 'gate_w': gate_w, 'gate_b': gate_b, 'ln_g': ln_g, 'ln_b': ln_b}
    _L0_attn_in = _L0_attn_setup()

    def _L0_ffn_setup():
        import jax, jax.numpy as jnp
        import numpy as np
        B, T, D, E, FF, K = (4, 128, 128, 8, 256, 2)
        SINKHORN_ITERS = 3

        def _sinkhorn(log_alpha, iters=SINKHORN_ITERS):
            for _ in range(iters):
                log_alpha = log_alpha - jax.nn.logsumexp(log_alpha, axis=-1, keepdims=True)
                log_alpha = log_alpha - jax.nn.logsumexp(log_alpha, axis=-2, keepdims=True)
            gates = jnp.exp(log_alpha)
            return gates / (jnp.sum(gates, axis=-1, keepdims=True) + 1e-08)
        key = jax.random.key(seed)
        ks = jax.random.split(key, 7)
        scale = 0.02
        return {'x': jax.random.normal(ks[0], (B, T, D), dtype=jnp.float32), 'router_w': jax.random.normal(ks[1], (E, D), dtype=jnp.float32) * scale, 'router_b': jnp.zeros((E,), dtype=jnp.float32), 'temperature': jnp.ones((1,), dtype=jnp.float32) * 0.5, 'wg': jax.random.normal(ks[2], (E, D, FF), dtype=jnp.float32) * scale, 'wp': jax.random.normal(ks[3], (E, D, FF), dtype=jnp.float32) * scale, 'wo': jax.random.normal(ks[4], (E, FF, D), dtype=jnp.float32) * scale}
    _L0_ffn_in = _L0_ffn_setup()
    _d = {'L0_attn_x': _L0_attn_in['x'], 'L0_attn_qkv_w': _L0_attn_in['qkv_w'], 'L0_attn_qkv_b': _L0_attn_in['qkv_b'], 'L0_attn_gate_w': _L0_attn_in['gate_w'], 'L0_attn_gate_b': _L0_attn_in['gate_b'], 'L0_attn_ln_g': _L0_attn_in['ln_g'], 'L0_attn_ln_b': _L0_attn_in['ln_b'], 'L0_ffn_router_w': _L0_ffn_in['router_w'], 'L0_ffn_router_b': _L0_ffn_in['router_b'], 'L0_ffn_temperature': _L0_ffn_in['temperature'], 'L0_ffn_wg': _L0_ffn_in['wg'], 'L0_ffn_wp': _L0_ffn_in['wp'], 'L0_ffn_wo': _L0_ffn_in['wo']}
    _x0 = _d['L0_attn_x']
    _d['L0_attn_x'] = jax.random.normal(jax.random.fold_in(jax.random.key(seed), 1), (8, 1024, 128), dtype=_x0.dtype)
    del _x0
    return _d

def reference(L0_attn_x, L0_attn_qkv_w, L0_attn_qkv_b, L0_attn_gate_w, L0_attn_gate_b, L0_attn_ln_g, L0_attn_ln_b, L0_ffn_router_w, L0_ffn_router_b, L0_ffn_temperature, L0_ffn_wg, L0_ffn_wp, L0_ffn_wo):

    def _L0_attn_ref(x, qkv_w, qkv_b, gate_w, gate_b, ln_g, ln_b):
        import jax, jax.numpy as jnp
        import numpy as np
        D_MODEL = 128
        LN_EPS = 1e-05
        DEN_EPS = 1e-06

        def _layer_norm(x, g, b):
            mu = jnp.mean(x, axis=-1, keepdims=True)
            var = jnp.mean(jnp.square(x - mu), axis=-1, keepdims=True)
            return (x - mu) * jax.lax.rsqrt(var + LN_EPS) * g + b
        B, T, D = x.shape
        xn = _layer_norm(x, ln_g, ln_b)
        qkv = xn @ qkv_w + qkv_b
        q, k, v = jnp.split(qkv, 3, axis=-1)
        gate = jax.nn.sigmoid(xn @ gate_w + gate_b)
        k = k * gate
        q = jax.nn.elu(q) + 1.0
        k = jax.nn.elu(k) + 1.0
        attn = jnp.einsum('btd,bsd->bts', q, k)
        mask = jnp.tril(jnp.ones((T, T), dtype=attn.dtype))
        attn = attn * mask
        out_num = jnp.einsum('bts,bsd->btd', attn, v)
        k_cumsum = jnp.cumsum(k, axis=1)
        out_den = jnp.sum(q * k_cumsum, axis=-1, keepdims=True) + DEN_EPS
        return out_num / out_den

    def _L0_ffn_ref(x, router_w, router_b, temperature, wg, wp, wo):
        import jax, jax.numpy as jnp
        import numpy as np
        B, T, D, E, FF, K = (4, 128, 128, 8, 256, 2)
        SINKHORN_ITERS = 3

        def _sinkhorn(log_alpha, iters=SINKHORN_ITERS):
            for _ in range(iters):
                log_alpha = log_alpha - jax.nn.logsumexp(log_alpha, axis=-1, keepdims=True)
                log_alpha = log_alpha - jax.nn.logsumexp(log_alpha, axis=-2, keepdims=True)
            gates = jnp.exp(log_alpha)
            return gates / (jnp.sum(gates, axis=-1, keepdims=True) + 1e-08)
        temp = jnp.maximum(temperature, 0.1)
        scores = (jnp.einsum('btd,ed->bte', x, router_w) + router_b) / temp
        gates = _sinkhorn(scores)
        topk_vals, topk_idx = jax.lax.top_k(gates, K)
        topk_gates = topk_vals / (jnp.sum(topk_vals, axis=-1, keepdims=True) + 1e-08)
        g = jax.nn.relu(jnp.einsum('btd,edf->btef', x, wg))
        p = jnp.einsum('btd,edf->btef', x, wp)
        all_out = jnp.einsum('btef,efd->bted', g * p, wo)
        gathered = jnp.take_along_axis(all_out, topk_idx[..., None], axis=2)
        expert_out = jnp.sum(gathered * topk_gates[..., None], axis=2)
        return x + expert_out
    x = L0_attn_x
    xn = _layernorm(x, axis=-1)
    x = x + _L0_attn_ref(xn, L0_attn_qkv_w, L0_attn_qkv_b, L0_attn_gate_w, L0_attn_gate_b, L0_attn_ln_g, L0_attn_ln_b) + _L0_ffn_ref(xn, L0_ffn_router_w, L0_ffn_router_b, L0_ffn_temperature, L0_ffn_wg, L0_ffn_wp, L0_ffn_wo)
    return x

_drawn_inputs = setup_inputs


def setup_inputs(seed=0):
    import zlib

    import numpy as np

    out = dict(_drawn_inputs(seed))
    spreads = {'L0_attn_ln_g': (1.0, 0.6), 'L0_attn_ln_b': (0.0, 0.691), 'L0_ffn_router_b': (0.0, 0.8)}
    factors = {'L0_attn_gate_w': 64.0,
     'L0_attn_gate_b': 64.0,
     'L0_ffn_router_w': 8.0,
     'L0_ffn_wg': 8.0,
     'L0_ffn_wp': 8.0,
     'L0_ffn_wo': 8.0,
     'L0_attn_qkv_w': 3.398,
     'L0_attn_qkv_b': 5.718}
    for name, (base, spread) in spreads.items():
        noise = np.random.default_rng([zlib.crc32(name.encode()), seed]).standard_normal(out[name].shape)
        drawn = base * np.exp(spread * noise) if base else spread * noise
        out[name] = jnp.asarray(drawn.astype(out[name].dtype))
    for name, factor in factors.items():
        out[name] = (out[name] * factor).astype(out[name].dtype)
    return out
```

```python
from contextlib import ExitStack

import concourse.bass as bass
from concourse import mybir

F32 = mybir.dt.float32
ALU = mybir.AluOpType
ACT = mybir.ActivationFunctionType
AX_X = mybir.AxisListType.X

LN_EPS = 1e-5
DEN_EPS = 1e-6
GATE_EPS = 1e-8
SINKHORN_ITERS = 3
TEMP_MIN = 0.1
BIG = 4.0


def sparse_block_kernel(nc, x, qkv_w, qkv_b, gate_w, gate_b, ln_g, ln_b,
                        router_w, router_b, temperature, wg, wp, wo, out):
    P = nc.NUM_PARTITIONS
    B, T, D = x.shape
    E, _, FF = wg.shape
    C = T // P
    NT = B * C
    G = 4
    GW = G * P
    NG = NT // G
    GB = C // G
    D1 = D + 1
    FB = FF // P
    assert D == P and C == 8 and GB == 2 and FB == 2

    x_view = x.rearrange("b (c p) d -> b p c d", p=P)
    out_view = out.rearrange("b (c p) d -> p (b c) d", p=P)

    with ExitStack() as ctx:
        def sb(name, shape, dt=F32):
            return ctx.enter_context(nc.sbuf_tensor(name, shape, dt))

        def sem(name):
            return ctx.enter_context(nc.semaphore(name))

        xs = sb("xs", [P, NT, D])
        zT = sb("zT", [P, NT, P])
        ident = sb("ident", [P, P])
        ones = sb("ones", [P, P])
        causal = sb("causal", [P, P])
        mean = sb("mean", [P, NT])
        rstd1 = sb("rstd1", [P, NT])
        std2 = sb("std2", [P, NT])
        mr = sb("mr", [P, NT])
        r1p = sb("r1p", [P, NT])
        gate = sb("gate", [P, NT, E])

        w_raw = sb("w_raw", [P, 4 * D])
        w_in = sb("w_in", [P, 4 * D])
        g_col = sb("g_col", [P, 1])
        b_col = sb("b_col", [P, 1])
        b_wide = sb("b_wide", [P, P])
        bias_in = sb("bias_in", [P, 4])
        bias_col = sb("bias_col", [P, 4])
        hbg = sb("hbg", [P, 1])
        hbk = sb("hbk", [P, 1])
        bv_raw = sb("bv_raw", [P, D])
        bv = sb("bv", [P, D])
        rw_raw = sb("rw_raw", [E, D])
        rwT = sb("rwT", [P, E])
        rb = sb("rb", [P, E])
        temp = sb("temp", [P, 1])
        temp_c = sb("temp_c", [P, 1])
        rtemp = sb("rtemp", [P, 1])
        w_gp = sb("w_gp", [P, E, 2 * FF])
        w_o = sb("w_o", [P, E, FB, D])

        stats = sb("stats", [P, C, 6])
        m_sum = sb("m_sum", [P, C])
        m_dif = sb("m_dif", [P, C])
        m_dif2 = sb("m_dif2", [P, C])
        m_sq = sb("m_sq", [P, C])
        mv = sb("mv", [P, 2, C])
        va = sb("va", [P, 2, C])
        ra = sb("ra", [P, C])
        v2 = sb("v2", [P, C])
        sq = sb("sq", [P, 2, C])
        rs = sb("rs", [P, 2, C])
        r12 = sb("r12", [P, C])
        z = sb("z", [P, 2, G, D])
        zTg = sb("zTg", [P, 2, G, P])

        rA = sb("rA", [P, NT, E])
        rB = sb("rB", [P, NT, E])
        rC = sb("rC", [P, NT, E])
        rank = sb("rank", [P, E])
        t64 = sb("t64", [P, NT])
        u64 = sb("u64", [P, NT])
        v64 = sb("v64", [P, NT])
        cmax = sb("cmax", [NT, 1])
        diag = sb("diag", [NT, NT])

        xr = sb("xr", [P, G, D])
        th = sb("th", [P, GW])
        sg = sb("sg", [P, GW])
        kg = sb("kg", [P, GW])
        ek = sb("ek", [P, GW])
        rk = sb("rk", [P, GW])
        eq = sb("eq", [P, GW])
        rq = sb("rq", [P, GW])
        kp = sb("kp", [P, 2, G, P])
        qp = sb("qp", [P, 2, G, P])
        v1 = sb("v1", [P, 2, G, D1])
        ktok = sb("ktok", [P, G, P])
        scores = sb("scores", [P, 2, G, P])
        state = sb("state", [P, C, D1])
        den = sb("den", [P, G])
        rden = sb("rden", [P, G])

        xT = sb("xT", [P, 2, P])
        relu = sb("relu", [P, 2, FF])
        h = sb("h", [P, 2, FF])
        hT = sb("hT", [P, 2, FB, P])

        psum = ctx.enter_context(nc.psum_tensor("psum", [P, 8, 512], F32))

        x_in = [sem("x_in0"), sem("x_in1")]
        w_loaded = sem("w_loaded")
        ew_loaded = sem("ew_loaded")
        const_ready = sem("const_ready")
        prep_pe = sem("prep_pe")
        prep_dve = sem("prep_dve")
        stat_step = sem("stat_step")
        sqrt_in = sem("sqrt_in")
        sqrt_out = sem("sqrt_out")
        z_ready = sem("z_ready")
        zT_ready = sem("zT_ready")
        zT_saved = sem("zT_saved")
        zT_kept = sem("zT_kept")
        logit_ready = sem("logit_ready")
        logit_saved = sem("logit_saved")
        route_dve = sem("route_dve")
        route_act = sem("route_act")
        route_pe = sem("route_pe")
        base_ready = sem("base_ready")
        za_ready = sem("za_ready")
        g_ready = sem("g_ready")
        k_ready = sem("k_ready")
        q_ready = sem("q_ready")
        v_ready = sem("v_ready")
        th_done = sem("th_done")
        sg_done = sem("sg_done")
        xr_done = sem("xr_done")
        kg_done = sem("kg_done")
        ek_done = sem("ek_done")
        kp_done = sem("kp_done")
        rq_done = sem("rq_done")
        qp_done = sem("qp_done")
        v_saved = sem("v_saved")
        a_ready = sem("a_ready")
        a_masked = sem("a_masked")
        kt_ready = sem("kt_ready")
        kt_saved = sem("kt_saved")
        s_ready = sem("s_ready")
        s_saved = sem("s_saved")
        o_ready = sem("o_ready")
        o_used = sem("o_used")
        rden_step = sem("rden_step")
        attn_done = sem("attn_done")
        xT_ready = sem("xT_ready")
        gu_ready = sem("gu_ready")
        relu_done = sem("relu_done")
        h_done = sem("h_done")
        hT_ready = sem("hT_ready")
        hT_saved = sem("hT_saved")
        wo_done = sem("wo_done")
        y_added = sem("y_added")
        stored = sem("stored")

        def wait(eng, s, value):
            if not isinstance(value, int) or value > 0:
                eng.wait_ge(s, value)

        def loop_and_last(eng, n, body):
            with eng.Fori(0, n - 1) as i:
                body(i, False)
            body(n - 1, True)

        WQ, WK, WV, WG = (slice(i * D, (i + 1) * D) for i in range(4))
        PAIRS = B // 2
        ROUND = 11
        ROW_SHIFTED, ROW_SUMMED, TOKEN_MAX, DIAG, COL_SHIFTED, COL_SUMMED = 2, 3, 5, 7, 9, 10

        def route_step(s, place=0):
            return 2 + ROUND * s + place

        block = ctx.enter_context(nc.Block())

        @block.sync
        def _(sp):
            with sp.Fori(0, PAIRS) as i:
                for j in range(2):
                    sp.wait_ge(x_in[j], 16 * i)
                    sp.dma_start(xs[:, bass.ds((2 * i + j) * C, C), :], x_view[bass.ds(2 * i + j, 1)]
                                 .rearrange("a p c d -> p (a c) d")).then_inc(x_in[j], 16)
            sp.dma_start(w_gp[:, :, 0:FF], wg.rearrange("e d f -> d e f")).then_inc(ew_loaded, 16)
            sp.dma_start(w_gp[:, :, FF:2 * FF], wp.rearrange("e d f -> d e f")).then_inc(ew_loaded, 16)
            sp.dma_start(w_o[:, :, :, :], wo.rearrange("e (b p) d -> p e b d", p=P)).then_inc(ew_loaded, 16)
            with sp.Fori(0, NT // 2) as i:
                sp.wait_ge(y_added, 2 * i + 2)
                sp.dma_start(out_view[:, bass.ds(2 * i, 2), :], xs[:, bass.ds(2 * i, 2), :]).then_inc(stored, 16)
            sp.wait_ge(stored, 16 * (NT // 2))

        @block.gpsimd
        def _(pool):
            pool.memset(ones[:], 1.0).then_inc(const_ready, 1)
            pool.memset(ident[:], 0.0).then_inc(const_ready, 1)
            pool.memset(causal[:], 1.0).then_inc(const_ready, 1)
            pool.memset(v1[:], 1.0).then_inc(const_ready, 1)
            pool.iota(rank[:], pattern=[[-1, E]], base=E, channel_multiplier=0,
                      allow_small_or_imprecise_dtypes=True).then_inc(const_ready, 1)
            pool.wait_ge(const_ready, 5)
            pool.affine_select(out=ident[:], in_=ident[:], compare_op=ALU.not_equal, fill=1.0, base=0,
                               pattern=[[-1, P]], channel_multiplier=1).then_inc(const_ready, 1)
            pool.affine_select(out=causal[:], in_=causal[:], compare_op=ALU.is_ge, fill=0.0, base=0,
                               pattern=[[1, P]], channel_multiplier=-1).then_inc(const_ready, 1)

            with pool.Fori(0, PAIRS) as i:
                for gl in range(2 * GB):
                    n = 2 * GB * i + gl
                    pool.wait_ge(zT_saved, n + 1)
                    pool.tensor_copy(zT[:, bass.ds(n * G, G), :], zTg[:, gl % 2]).then_inc(zT_kept, 1)

            def fetch_zT(n, hb):
                wait(pool, v_ready, n - 1)
                pool.tensor_copy(zTg[:, hb], zT[:, bass.ds(n * G, G), :]).then_inc(za_ready, 1)

            def group(n, hb, is_last):
                pool.wait_ge(th_done, n + 1)
                wait(pool, kg_done, n)
                pool.tensor_tensor(sg[:], th[:], ones[:, 0:1].to_broadcast([P, GW]), ALU.add).then_inc(sg_done, 1)
                if not is_last:
                    fetch_zT(n + 1, 1 - hb)
                tiles = bass.ds(n * G, G)
                wait(pool, base_ready, n)
                pool.tensor_tensor(xr[:], xs[:, tiles, :], r1p[:, tiles].unsqueeze(2).to_broadcast([P, G, D]),
                                   ALU.mult).then_inc(xr_done, 1)
                pool.wait_ge(xr_done, n + 1)
                pool.tensor_tensor(xs[:, tiles, :], xr[:], mr[:, tiles].unsqueeze(2).to_broadcast([P, G, D]),
                                   ALU.subtract).then_inc(base_ready, 1)

            pool.wait_ge(zT_kept, NG)
            pool.wait_ge(logit_ready, B)
            pool.wait_ge(prep_dve, 6)
            fetch_zT(0, 0)
            group(0, 0, False)

            def pair(m, is_last):
                group(2 * m + 1, 1, is_last)
                if not is_last:
                    group(2 * m + 2, 0, False)
            with pool.Fori(0, NG // 2 - 1) as m:
                pair(m, False)
            pair(NG // 2 - 1, True)

            def tile(i, j):
                wait(pool, gu_ready, (i - 1) * E)
                pool.tensor_copy(xT[:, j, :], zT[:, bass.ds(i, 1), :]).then_inc(xT_ready, 1)
            tile(0, 0)
            tile(1, 1)
            with pool.Fori(1, NT // 2) as i:
                for j in range(2):
                    tile(2 * i + j, j)

        @block.scalar
        def _(act):
            act.dma_start(w_raw[:, 0:3 * D], qkv_w).then_inc(w_loaded, 16)
            act.dma_start(w_raw[:, WG], gate_w).then_inc(w_loaded, 16)
            act.dma_start(g_col[:], ln_g.rearrange("(p a) -> p a", a=1)).then_inc(w_loaded, 16)
            act.dma_start(b_col[:], ln_b.rearrange("(p a) -> p a", a=1)).then_inc(w_loaded, 16)
            act.dma_start(bias_in[:, 0:3], qkv_b.rearrange("(a p) -> p a", p=P), allow_slow_non_contiguous=True).then_inc(w_loaded, 16)
            act.dma_start(bias_in[:, 3:4], gate_b.rearrange("(p a) -> p a", a=1)).then_inc(w_loaded, 16)
            act.dma_start(bv_raw[:], qkv_b[2 * D:3 * D].partition_broadcast(P)).then_inc(w_loaded, 16)
            act.dma_start(rw_raw[:], router_w).then_inc(w_loaded, 16)
            act.dma_start(rb[:], router_b.partition_broadcast(P)).then_inc(w_loaded, 16)
            act.dma_start(temp[:], temperature.partition_broadcast(P)).then_inc(w_loaded, 16)

            with act.Fori(0, PAIRS) as i:
                for gl in range(2 * GB):
                    n = 2 * GB * i + gl
                    if gl % GB == 0:
                        b = 2 * i + gl // GB
                        act.wait_ge(sqrt_in, b + 1)
                        act.activation(sq[:], va[:], ACT.Sqrt).then_inc(sqrt_out, 1)
                    act.wait_ge(zT_ready, n + 1)
                    wait(act, zT_kept, n - 1)if gl >= 2 else act.wait_ge(zT_kept, 4 * i)
                    act.wait_ge(logit_ready, (2 * i + gl // GB))
                    act.activation(zTg[:, gl % 2], psum[:, gl % 2, :].rearrange("p (g t) -> p g t", g=G),
                                   ACT.Copy).then_inc(zT_saved, 1)

            for s in range(SINKHORN_ITERS):
                act.wait_ge(route_dve, route_step(s, ROW_SHIFTED))
                act.activation(rB[:], rA[:], ACT.Exp).then_inc(route_act, 1)
                act.wait_ge(route_dve, route_step(s, ROW_SUMMED))
                act.activation(u64[:], t64[:], ACT.Ln).then_inc(route_act, 1)
                act.wait_ge(route_dve, route_step(s, COL_SHIFTED))
                act.activation(rB[:], rA[:], ACT.Exp).then_inc(route_act, 1)
                act.wait_ge(route_pe, 3 * s + 3)
                act.activation(u64[:], psum[:, 2, 0:NT], ACT.Ln).then_inc(route_act, 1)
            act.wait_ge(route_dve, route_step(SINKHORN_ITERS))
            act.activation(rB[:], rC[:], ACT.Exp).then_inc(route_act, 1)

            def tanh_gate(n):
                act.wait_ge(g_ready, n + 1)
                wait(act, sg_done, n)
                act.activation(th[:], psum[:, 0, :], ACT.Tanh, bias=hbg[:], scale=0.5).then_inc(th_done, 1)

            def exp_query(n):
                act.wait_ge(q_ready, n + 1)
                wait(act, qp_done, n)
                act.activation(eq[:], psum[:, 2, :], ACT.Exp, bias=bias_col[:, 0:1])
                act.activation(rq[:], psum[:, 2, :], ACT.Relu, bias=bias_col[:, 0:1]).then_inc(rq_done, 1)

            def exp_key(n):
                act.wait_ge(kg_done, n + 1)
                wait(act, kp_done, n)
                act.activation(ek[:], kg[:], ACT.Exp)
                act.activation(rk[:], kg[:], ACT.Relu).then_inc(ek_done, 1)

            def copy_state(b, hb, c):
                cb = G * hb + c
                if cb == C - 1:
                    return
                act.wait_ge(s_ready, (C - 1) * b + cb + 1)
                wait(act, o_ready, GB * b + hb + (1 if cb + 1 == G else 0))
                act.activation(state[:, cb + 1, :], psum[:, 5, 0:D1], ACT.Copy).then_inc(s_saved, 1)

            def batch(b, is_last):
                for hb in range(GB):
                    n = GB * b + hb
                    ahead = not (is_last and hb == GB - 1)
                    act.wait_ge(kt_ready, n + 1)
                    wait(act, s_ready, (C - 1) * b + G * hb)
                    act.activation(ktok[:], psum[:, 3, :].rearrange("p (g t) -> p g t", g=G), ACT.Copy)\
                       .then_inc(kt_saved, 1)
                    copy_state(b, hb, 0)
                    if ahead:
                        tanh_gate(n + 1)
                    copy_state(b, hb, 1)
                    copy_state(b, hb, 2)
                    if ahead:
                        exp_query(n + 1)
                        exp_key(n + 1)
                    copy_state(b, hb, 3)

            act.wait_ge(prep_dve, 6)
            tanh_gate(0)
            exp_query(0)
            exp_key(0)
            loop_and_last(act, B, batch)

            def saved_hT(k, kb):
                act.wait_ge(hT_ready, k + 1)
                wait(act, wo_done, k - 1)
                act.activation(hT[:, kb], psum[:, 2 + kb, 0:FF].rearrange("p (b t) -> p b t", b=FB),
                               ACT.Copy).then_inc(hT_saved, 1)

            def expert(i, e, first):
                k = i * E + e
                act.wait_ge(gu_ready, k + 1)
                wait(act, h_done, k - 1)
                act.activation(relu[:, e % 2, :], psum[:, e % 2, 0:FF], ACT.Relu,
                               scale=gate[:, bass.ds(i, 1), e]).then_inc(relu_done, 1)
                if not first:
                    saved_hT(k - 1, (e - 1) % 2)
            for e in range(E):
                expert(0, e, e == 0)
            with act.Fori(1, NT) as i:
                for e in range(E):
                    expert(i, e, False)
            saved_hT(NT * E - 1, 1)

        @block.vector
        def _(dve):
            dve.wait_ge(w_loaded, 16 * 10)
            dve.wait_ge(const_ready, 7)
            dve.tensor_scalar(w_in[:, WQ], w_raw[:, WQ], g_col[:], None, ALU.mult)
            dve.tensor_scalar(w_in[:, 2 * D:4 * D], w_raw[:, 2 * D:4 * D], g_col[:], None, ALU.mult)\
               .then_inc(prep_dve, 1)
            dve.tensor_scalar(b_wide[:], ones[:], b_col[:], None, ALU.mult)
            dve.tensor_scalar(w_in[:, WK], w_raw[:, WK], g_col[:], 0.5, ALU.mult, ALU.mult).then_inc(prep_dve, 1)
            dve.wait_ge(prep_pe, 1)
            dve.tensor_tensor(bias_col[:], psum[:, 0, 0:4], bias_in[:], ALU.add).then_inc(prep_dve, 1)
            dve.tensor_tensor(bv[:], psum[:, 1, 0:D], bv_raw[:], ALU.add)
            dve.tensor_copy(rwT[:], psum[:, 2, 0:E])
            dve.tensor_scalar(temp_c[:], temp[:], TEMP_MIN, None, ALU.max).then_inc(prep_dve, 1)
            dve.wait_ge(prep_dve, 4)
            dve.tensor_scalar(hbg[:], bias_col[:, 3:4], 0.5, None, ALU.mult)
            dve.tensor_scalar(hbk[:], bias_col[:, 1:2], 0.5, None, ALU.mult)
            dve.reciprocal(rtemp[:], temp_c[:]).then_inc(prep_dve, 1)

            STEPS = 9
            with dve.Fori(0, PAIRS) as i:
                for j in range(2):
                    b = 2 * i + j
                    done = STEPS * b
                    tiles = bass.ds(b * C, C)
                    dve.wait_ge(x_in[j], 16 * (i + 1))
                    for c in range(C):
                        last = dve.bn_stats(stats[:, c, :], xs[:, bass.ds(b * C + c, 1), :]
                                            .rearrange("p a d -> p (a d)"))
                    last.then_inc(stat_step, 1)
                    dve.wait_ge(stat_step, done + 1)
                    dve.tensor_tensor(m_sum[:], stats[:, :, 1], stats[:, :, 4], ALU.add)
                    dve.tensor_tensor(m_dif[:], stats[:, :, 1], stats[:, :, 4], ALU.subtract)
                    dve.tensor_tensor(m_sq[:], stats[:, :, 2], stats[:, :, 5], ALU.add).then_inc(stat_step, 1)
                    dve.wait_ge(stat_step, done + 2)
                    dve.scalar_tensor_tensor(m_dif2[:], m_dif[:], 0.25, m_dif[:], ALU.mult, ALU.mult)
                    dve.tensor_scalar(mv[:, 0, :], m_sum[:], 0.5, None, ALU.mult).then_inc(stat_step, 1)
                    dve.wait_ge(stat_step, done + 3)
                    dve.scalar_tensor_tensor(mv[:, 1, :], m_sq[:], 1.0 / D, m_dif2[:], ALU.mult, ALU.add)\
                       .then_inc(stat_step, 1)
                    dve.tensor_copy(mean[:, tiles], mv[:, 0, :])
                    dve.wait_ge(stat_step, done + 4)
                    dve.tensor_scalar(va[:, 0, :], mv[:, 1, :], LN_EPS, None, ALU.add).then_inc(stat_step, 1)
                    dve.wait_ge(stat_step, done + 5)
                    dve.reciprocal(ra[:], va[:, 0, :]).then_inc(stat_step, 1)
                    dve.wait_ge(stat_step, done + 6)
                    dve.tensor_tensor(v2[:], mv[:, 1, :], ra[:], ALU.mult).then_inc(stat_step, 1)
                    dve.wait_ge(stat_step, done + 7)
                    dve.tensor_scalar(va[:, 1, :], v2[:], LN_EPS, None, ALU.add).then_inc(sqrt_in, 1)
                    dve.wait_ge(sqrt_out, b + 1)
                    dve.reciprocal(rs[:], sq[:]).then_inc(stat_step, 1)
                    dve.tensor_copy(std2[:, tiles], sq[:, 1, :])
                    dve.wait_ge(stat_step, done + 8)
                    dve.tensor_tensor(r12[:], rs[:, 0, :], rs[:, 1, :], ALU.mult).then_inc(stat_step, 1)
                    dve.tensor_copy(rstd1[:, tiles], rs[:, 0, :])
                    dve.wait_ge(stat_step, done + 9)
                    for gl in range(GB):
                        n = GB * b + gl
                        dve.wait_ge(zT_ready, GB * b)
                        for t in range(G):
                            c = G * gl + t
                            last = dve.tensor_scalar(z[:, gl, t, :],
                                                     xs[:, bass.ds(b * C + c, 1), :].rearrange("p a d -> p (a d)"),
                                                     mv[:, 0, c:c + 1], r12[:, c:c + 1], ALU.subtract, ALU.mult)
                        last.then_inc(z_ready, 1)
                    dve.wait_ge(logit_ready, b + 1)
                    dve.tensor_tensor(gate[:, tiles, :], psum[:, 2 + j, 0:C * E].rearrange("p (c e) -> p c e", e=E),
                                      std2[:, tiles].unsqueeze(2).to_broadcast([P, C, E]), ALU.mult)\
                       .then_inc(logit_saved, 1)

            chain = [0]

            def link(ins):
                chain[0] += 1
                ins.then_inc(route_dve, 1)
                dve.wait_ge(route_dve, chain[0])

            def over_e(a):
                return a.unsqueeze(2).to_broadcast([P, NT, E])

            def by_batch(a):
                return a.rearrange("p (b c) e -> p b c e", c=C)

            def over_c(a):
                return a.rearrange("p (b e) -> p b e", e=E).unsqueeze(2).to_broadcast([P, B, C, E])

            dve.wait_ge(prep_dve, 5)
            dve.wait_ge(logit_saved, B)
            dve.tensor_tensor(mr[:], mean[:], rstd1[:], ALU.mult)
            dve.tensor_scalar(r1p[:], rstd1[:], 1.0, None, ALU.add).then_inc(prep_dve, 1)
            link(dve.tensor_tensor(rA[:], gate[:], rb[:].unsqueeze(1).to_broadcast([P, NT, E]), ALU.add))
            link(dve.tensor_scalar(rC[:], rA[:], rtemp[:], None, ALU.mult))
            acts = 0
            for s in range(SINKHORN_ITERS):
                link(dve.tensor_reduce(t64[:], rC[:], AX_X, ALU.max))
                link(dve.tensor_tensor(rA[:], rC[:], over_e(t64[:]), ALU.subtract))
                acts += 1
                dve.wait_ge(route_act, acts)
                link(dve.tensor_reduce(t64[:], rB[:], AX_X, ALU.add))
                acts += 1
                dve.wait_ge(route_act, acts)
                link(dve.tensor_tensor(rC[:], rA[:], over_e(u64[:]), ALU.subtract))
                link(dve.tensor_reduce(t64[:].rearrange("p (b e) -> p b e", e=E),
                                       by_batch(rC[:]).rearrange("p b c e -> p b e c"), AX_X, ALU.max))
                dve.wait_ge(route_pe, 3 * s + 1)
                link(dve.tensor_reduce(cmax[:], psum[0:NT, 0, 0:P], AX_X, ALU.max))
                link(dve.tensor_scalar(diag[:], ident[0:NT, 0:NT], cmax[:], None, ALU.mult))
                dve.wait_ge(route_pe, 3 * s + 2)
                link(dve.tensor_copy(v64[:], psum[:, 1, 0:NT]))
                link(dve.tensor_tensor(by_batch(rA[:]), by_batch(rC[:]), over_c(v64[:]), ALU.subtract))
                acts += 1
                dve.wait_ge(route_act, acts)
                link(dve.tensor_reduce(t64[:].rearrange("p (b e) -> p b e", e=E),
                                       by_batch(rB[:]).rearrange("p b c e -> p b e c"), AX_X, ALU.add))
                acts += 1
                dve.wait_ge(route_act, acts)
                link(dve.tensor_tensor(by_batch(rC[:]), by_batch(rA[:]), over_c(u64[:]), ALU.subtract))
                assert chain[0] == route_step(s + 1)
            acts += 1
            dve.wait_ge(route_act, acts)
            link(dve.tensor_reduce(t64[:], rB[:], AX_X, ALU.add))
            link(dve.tensor_scalar(u64[:], t64[:], GATE_EPS, None, ALU.add))
            link(dve.reciprocal(v64[:], u64[:]))
            link(dve.tensor_tensor(gate[:], rB[:], over_e(v64[:]), ALU.mult))
            ranks = rank[:].unsqueeze(1).to_broadcast([P, NT, E])

            def top(src, vmax, onehot):
                link(dve.tensor_reduce(vmax, src, AX_X, ALU.max))
                link(dve.tensor_tensor(rB[:], src, over_e(vmax), ALU.is_ge))
                link(dve.tensor_tensor(rB[:], rB[:], ranks, ALU.mult))
                link(dve.tensor_reduce(v64[:], rB[:], AX_X, ALU.max))
                link(dve.tensor_tensor(onehot, rB[:], over_e(v64[:]), ALU.is_equal))

            top(gate[:], t64[:], rA[:])
            link(dve.scalar_tensor_tensor(rC[:].rearrange("p t e -> p (t e)"), rA[:].rearrange("p t e -> p (t e)"),
                                          -BIG, gate[:].rearrange("p t e -> p (t e)"), ALU.mult, ALU.add))
            top(rC[:], u64[:], rC[:])
            link(dve.tensor_tensor(rA[:], rA[:], rC[:], ALU.add))
            link(dve.tensor_tensor(t64[:], t64[:], u64[:], ALU.add))
            link(dve.tensor_scalar(t64[:], t64[:], GATE_EPS, None, ALU.add))
            link(dve.reciprocal(u64[:], t64[:]))
            link(dve.tensor_tensor(u64[:], u64[:], std2[:], ALU.mult))
            link(dve.tensor_tensor(u64[:], u64[:], std2[:], ALU.mult))
            link(dve.tensor_tensor(rA[:], rA[:], over_e(u64[:]), ALU.mult))
            link(dve.tensor_tensor(gate[:], gate[:], rA[:], ALU.mult))

            def finish(n):
                dve.wait_ge(o_ready, n + 2)
                for j in range(2):
                    o2 = psum[:, 6 + j, 0:2 * D1].rearrange("p (k x) -> p k x", x=D1)
                    last = dve.tensor_scalar(den[:, 2 * j:2 * j + 2].unsqueeze(2), o2[:, :, D:D1], DEN_EPS, None,
                                             ALU.add)
                last.then_inc(rden_step, 1)
                dve.wait_ge(rden_step, 2 * n + 1)
                dve.reciprocal(rden[:], den[:]).then_inc(rden_step, 1)
                dve.wait_ge(rden_step, 2 * n + 2)
                dve.wait_ge(base_ready, n + 1)
                for t in range(G):
                    o = psum[:, 6 + t // 2, (t % 2) * D1:(t % 2) * D1 + D]
                    acc = xs[:, bass.ds(n * G + t, 1), :].rearrange("p a d -> p (a d)")
                    last = dve.scalar_tensor_tensor(acc, o, rden[:, t:t + 1], acc, ALU.mult, ALU.add)
                last.then_inc(o_used, 1)

            def group(n, hb):
                dve.wait_ge(k_ready, n + 1)
                dve.wait_ge(sg_done, n + 1)
                wait(dve, ek_done, n)
                dve.scalar_tensor_tensor(kg[:], psum[:, 1, :], hbk[:], sg[:], ALU.add, ALU.mult)\
                   .then_inc(kg_done, 1)
                dve.wait_ge(rq_done, n + 1)
                wait(dve, o_ready, n)
                dve.scalar_tensor_tensor(qp[:, hb].rearrange("p g t -> p (g t)"), eq[:], 1.0, rq[:],
                                         ALU.min, ALU.add).then_inc(qp_done, 1)
                dve.wait_ge(ek_done, n + 1)
                dve.scalar_tensor_tensor(kp[:, hb].rearrange("p g t -> p (g t)"), ek[:], 1.0, rk[:],
                                         ALU.min, ALU.add).then_inc(kp_done, 1)
                dve.wait_ge(v_ready, n + 1)
                dve.tensor_tensor(v1[:, hb, :, 0:D], psum[:, 3, :].rearrange("p (g d) -> p g d", g=G),
                                  bv[:].unsqueeze(1).to_broadcast([P, G, D]), ALU.add).then_inc(v_saved, 1)

            def mask(n, hb):
                dve.wait_ge(a_ready, n + 1)
                dve.tensor_tensor(scores[:, hb], psum[:, 4, :].rearrange("p (g t) -> p g t", g=G),
                                  causal[:].unsqueeze(1).to_broadcast([P, G, P]), ALU.mult).then_inc(a_masked, 1)

            dve.sem_inc(o_ready, 1)
            group(0, 0)
            mask(0, 0)
            group(1, 1)
            finish(0)
            mask(1, 1)
            with dve.Fori(1, B) as b:
                for hb in range(GB):
                    n = GB * b + hb
                    group(n, hb)
                    finish(n - 1)
                    mask(n, hb)
            finish(NG - 1)

            def expert(i, e):
                k = i * E + e
                dve.wait_ge(relu_done, k + 1)
                wait(dve, hT_ready, k - 1)
                dve.tensor_tensor(h[:, e % 2, :], relu[:, e % 2, :], psum[:, e % 2, FF:2 * FF], ALU.mult)\
                   .then_inc(h_done, 1)

            def add_tile(i, j):
                dve.wait_ge(wo_done, (i + 1) * E)
                acc = xs[:, bass.ds(i, 1), :].rearrange("p a d -> p (a d)")
                dve.tensor_tensor(acc, acc, psum[:, 4 + j, 0:D], ALU.add).then_inc(y_added, 1)

            def two_tiles(i, first):
                for j in range(2):
                    for e in range(E):
                        expert(2 * i + j, e)
                        if e == 3 and not (first and j == 0):
                            add_tile(2 * i + j - 1, 1 - j)
            dve.wait_ge(o_used, NG)
            two_tiles(0, True)
            with dve.Fori(1, NT // 2) as i:
                two_tiles(i, False)
            add_tile(NT - 1, 1)

        @block.tensor
        def _(pe):
            pe.wait_ge(w_loaded, 16 * 10)
            pe.wait_ge(const_ready, 7)
            pe.wait_ge(prep_dve, 2)
            for f in range(4):
                pe.matmul(psum[:, 0, f:f + 1], w_raw[:, f * D:(f + 1) * D], b_col[:], start=True, stop=True)
            pe.matmul(psum[:, 1, 0:D], b_wide[:], w_raw[:, WV], start=True, stop=True)
            pe.transpose(psum[:, 2, 0:E], rw_raw[:], ident[0:E, 0:E]).then_inc(prep_pe, 1)
            pe.wait_ge(prep_dve, 4)

            with pe.Fori(0, PAIRS) as i:
                for gl in range(2 * GB):
                    n = 2 * GB * i + gl
                    j = gl // GB
                    pe.wait_ge(z_ready, n + 1)
                    wait(pe, zT_saved, n - 1) if gl >= 2 else pe.wait_ge(zT_saved, 4 * i)
                    for t in range(G):
                        last = pe.transpose(psum[:, gl % 2, t * P:(t + 1) * P], z[:, gl % 2, t, :], ident[:])
                    last.then_inc(zT_ready, 1)
                    pe.wait_ge(zT_saved, n + 1)
                    if gl % GB == 0:
                        pe.wait_ge(logit_saved, 2 * i)
                    for t in range(G):
                        c = G * (gl % GB) + t
                        last = pe.matmul(psum[:, 2 + j, c * E:(c + 1) * E], zTg[:, gl % 2, t, :], rwT[:],
                                         start=True, stop=True)
                    if gl % GB == GB - 1:
                        last.then_inc(logit_ready, 1)

            for s in range(SINKHORN_ITERS):
                pe.wait_ge(route_dve, route_step(s, TOKEN_MAX))
                pe.transpose(psum[0:NT, 0, 0:P], t64[:], ident[:]).then_inc(route_pe, 1)
                pe.wait_ge(route_dve, route_step(s, DIAG))
                pe.matmul(psum[:, 1, 0:NT], ones[0:NT, :], diag[:], start=True, stop=True).then_inc(route_pe, 1)
                pe.wait_ge(route_dve, route_step(s, COL_SUMMED))
                pe.matmul(psum[:, 2, 0:NT], ones[:], t64[:], start=True, stop=True).then_inc(route_pe, 1)
            pe.wait_ge(route_act, 4 * SINKHORN_ITERS)

            def project(n, hb, what):
                zt = zTg[:, hb].rearrange("p g t -> p (g t)")
                if what == "g":
                    pe.wait_ge(za_ready, n + 1)
                    wait(pe, th_done, n)
                    pe.matmul(psum[:, 0, :], w_in[:, WG], zt, start=True, stop=True).then_inc(g_ready, 1)
                if what == "k":
                    wait(pe, kg_done, n)
                    pe.matmul(psum[:, 1, :], w_in[:, WK], zt, start=True, stop=True).then_inc(k_ready, 1)
                if what == "q":
                    wait(pe, rq_done, n)
                    pe.matmul(psum[:, 2, :], w_in[:, WQ], zt, start=True, stop=True).then_inc(q_ready, 1)
                if what == "v":
                    wait(pe, kt_saved, n)
                    for t in range(G):
                        last = pe.matmul(psum[:, 3, t * D:(t + 1) * D], zTg[:, hb, t, :], w_in[:, WV],
                                         start=True, stop=True)
                    last.then_inc(v_ready, 1)

            def group(b, hb, last_group):
                n = GB * b + hb
                pe.wait_ge(kp_done, n + 1)
                pe.wait_ge(qp_done, n + 1)
                wait(pe, a_masked, n)
                for c in range(G):
                    last = pe.matmul(psum[:, 4, c * P:(c + 1) * P], kp[:, hb, c, :], qp[:, hb, c, :],
                                     start=True, stop=True)
                last.then_inc(a_ready, 1)
                pe.wait_ge(v_saved, n + 1)
                for c in range(G):
                    last = pe.transpose(psum[:, 3, c * P:(c + 1) * P], kp[:, hb, c, :], ident[:])
                last.then_inc(kt_ready, 1)
                for c, what in enumerate("gkqv"):
                    cb = G * hb + c
                    if not last_group:
                        project(n + 1, 1 - hb, what)
                    if c == 0:
                        pe.wait_ge(kt_saved, n + 1)
                    if cb < C - 1:
                        wait(pe, s_saved, (C - 1) * b + cb)
                        pe.matmul(psum[:, 5, 0:D1], ktok[:, c, :], v1[:, hb, c, :],
                                  start=(cb == 0), stop=True, skip_group_check=True).then_inc(s_ready, 1)
                pe.wait_ge(a_masked, n + 1)
                wait(pe, o_used, n)
                for c in range(G):
                    cb = G * hb + c
                    o = psum[:, 6 + c // 2, (c % 2) * D1:(c % 2 + 1) * D1]
                    last = pe.matmul(o, scores[:, hb, c, :], v1[:, hb, c, :], start=True, stop=(cb == 0))
                    if cb > 0:
                        pe.wait_ge(s_saved, (C - 1) * b + cb)
                        last = pe.matmul(o, qp[:, hb, c, :], state[:, cb, :], start=False, stop=True)
                last.then_inc(o_ready, 1)

            for what in "gkqv":
                project(0, 0, what)

            def batch(b, is_last):
                for hb in range(GB):
                    group(b, hb, is_last and hb == GB - 1)
            loop_and_last(pe, B, batch)

            def up(k, i, e, j):
                if e == 0:
                    pe.wait_ge(xT_ready, i + 1)
                wait(pe, h_done, k - 1)
                pe.matmul(psum[:, e % 2, :], xT[:, j, :], w_gp[:, e, :], start=True, stop=True).then_inc(gu_ready, 1)

            def turn(k, e):
                pe.wait_ge(h_done, k + 1)
                wait(pe, hT_saved, k - 1)
                for f in range(FB):
                    last = pe.transpose(psum[:, 2 + e % 2, f * P:(f + 1) * P], h[:, e % 2, f * P:(f + 1) * P], ident[:])
                last.then_inc(hT_ready, 1)

            def down(k, i, e, j):
                pe.wait_ge(hT_saved, k + 1)
                if e == 0:
                    wait(pe, y_added, i - 1)
                for f in range(FB):
                    last = pe.matmul(psum[:, 4 + j, 0:D], hT[:, e % 2, f, :], w_o[:, e, f, :],
                                     start=(e == 0 and f == 0), stop=(e == E - 1 and f == FB - 1))
                last.then_inc(wo_done, 1)

            def two_tiles(i, is_last):
                for s in range(2 * E):
                    k = 2 * E * i + s
                    for ahead, stage in ((2, "up"), (1, "turn"), (0, "down")):
                        r = s + ahead
                        if is_last and r >= 2 * E:
                            continue
                        j, e = (r // E) % 2, r % E
                        if stage == "up":
                            up(k + 2, 2 * i + r // E, e, j)
                        elif stage == "turn":
                            turn(k + 1, e)
                        else:
                            down(k, 2 * i + j, e, j)
            pe.wait_ge(ew_loaded, 48)
            pe.wait_ge(o_used, NG)
            up(0, 0, 0, 0)
            up(1, 0, 1, 0)
            turn(0, 0)
            two_tiles(0, False)
            with pe.Fori(1, NT // 2 - 1) as i:
                two_tiles(i, False)
            two_tiles(NT // 2 - 1, True)


_INS = ["L0_attn_x", "L0_attn_qkv_w", "L0_attn_qkv_b", "L0_attn_gate_w", "L0_attn_gate_b", "L0_attn_ln_g",
        "L0_attn_ln_b", "L0_ffn_router_w", "L0_ffn_router_b", "L0_ffn_temperature", "L0_ffn_wg", "L0_ffn_wp",
        "L0_ffn_wo"]


def kernel(**inputs):
    import numpy as np
    import concourse.bacc as bacc
    from concourse.bass_utils import run_bass_kernel_spmd

    nc = bacc.Bacc("TRN2", target_bir_lowering=False, num_devices=1)
    arrays, args = {}, []
    for name in _INS:
        a = np.ascontiguousarray(inputs[name])
        arrays["in_" + name] = a
        args.append(nc.dram_tensor("in_" + name, a.shape, mybir.dt.from_np(a.dtype), kind="ExternalInput").ap())
    shape = arrays["in_L0_attn_x"].shape
    out = nc.dram_tensor("out", shape, F32, kind="ExternalOutput").ap()
    sparse_block_kernel(nc, *args, out)
    r = run_bass_kernel_spmd(nc, [arrays], core_ids=[0])
    return r.results[0]["out"]
```

```python
from contextlib import ExitStack

import concourse.bass as bass
from concourse import mybir

F32 = mybir.dt.float32
BF16 = mybir.dt.bfloat16
I32 = mybir.dt.int32
U32 = mybir.dt.uint32
ALU = mybir.AluOpType
ACT = mybir.ActivationFunctionType
AX_X = mybir.AxisListType.X

LN_EPS = 1e-5
DEN_EPS = 1e-6
GATE_EPS = 1e-8
SINKHORN_ITERS = 3
TEMP_MIN = 0.1
BIG = 4.0
AHEAD = 4


def sparse_block_kernel(nc, x, qkv_w, qkv_b, gate_w, gate_b, ln_g, ln_b,
                        router_w, router_b, temperature, wg, wp, wo, out):
    P = nc.NUM_PARTITIONS
    B, T, D = x.shape
    E, _, FF = wg.shape
    C = T // P
    NT = B * C
    G = 4
    GW = G * P
    NG = NT // G
    GB = C // G
    D1 = D + 1
    FB = FF // P
    NTOK = NT * P
    K = E * (E - 1) // 2
    TILES = 4
    NS = -(-(NT + K - 1) // TILES) * TILES
    ROW = D + 3
    KB = 7
    assert D == P and C == 8 and GB == 2 and FB == 2 and K % KB == 0 and KB * NT <= 512 and NS <= P

    x_view = x.rearrange("b (c p) d -> b p c d", p=P)
    out_view = out.rearrange("b (c p) d -> b p c d", p=P)
    sorted_rows = nc.dram_tensor("sorted_rows", (NS * P, ROW), F32).ap()
    expert_out = nc.dram_tensor("expert_out", (NTOK + NS * P, D), F32).ap()

    with ExitStack() as ctx:
        def sb(name, shape, dt=F32):
            return ctx.enter_context(nc.sbuf_tensor(name, shape, dt))

        def sem(name):
            return ctx.enter_context(nc.semaphore(name))

        xs = sb("xs", [P, NT, D])
        zT = sb("zT", [P, NT, P])
        rows = sb("rows", [P, NT, ROW])
        ident = sb("ident", [P, P])
        ones = sb("ones", [P, P])
        causal = sb("causal", [P, P])
        mean = sb("mean", [P, NT])
        rstd1 = sb("rstd1", [P, NT])
        std2 = sb("std2", [P, NT])
        var = sb("var", [P, NT])
        mr = sb("mr", [P, NT])
        r1p = sb("r1p", [P, NT])
        gate = sb("gate", [P, NT, E])

        w_raw = sb("w_raw", [P, 4 * D])
        w_in = sb("w_in", [P, 4 * D])
        g_col = sb("g_col", [P, 1])
        b_col = sb("b_col", [P, 1])
        b_wide = sb("b_wide", [P, P])
        bias_in = sb("bias_in", [P, 4])
        bias_col = sb("bias_col", [P, 4])
        hbg = sb("hbg", [P, 1])
        hbk = sb("hbk", [P, 1])
        bv_raw = sb("bv_raw", [P, D])
        bv = sb("bv", [P, D])
        rw_raw = sb("rw_raw", [E, D])
        rwT = sb("rwT", [P, E])
        rb = sb("rb", [P, E])
        temp = sb("temp", [P, 1])
        temp_c = sb("temp_c", [P, 1])
        rtemp = sb("rtemp", [P, 1])
        w_gp = sb("w_gp", [P, E, 2 * FF])
        w_o = sb("w_o", [P, E, FB, D])

        stats = sb("stats", [P, NT, 6])
        m_sum = sb("m_sum", [P, NT])
        m_dif = sb("m_dif", [P, NT])
        m_dif2 = sb("m_dif2", [P, NT])
        m_sq = sb("m_sq", [P, NT])
        va = sb("va", [P, 2, NT])
        ra = sb("ra", [P, NT])
        v2 = sb("v2", [P, NT])
        sq = sb("sq", [P, 2, NT])
        rs = sb("rs", [P, 2, NT])
        r12 = sb("r12", [P, NT])
        z = sb("z", [P, 2, G, D])
        zTg = sb("zTg", [P, 2, G, P])

        rA = sb("rA", [P, NT, E])
        rB = sb("rB", [P, NT, E])
        rC = sb("rC", [P, NT, E])
        rank = sb("rank", [P, E])
        t64 = sb("t64", [P, NT])
        u64 = sb("u64", [P, NT])
        v64 = sb("v64", [P, NT])
        cmax = sb("cmax", [NT, 1])
        diag = sb("diag", [NT, NT])

        place = sb("place", [P, NT])
        w_low = sb("w_low", [P, NT])
        w_high = sb("w_high", [P, NT])
        expert_no = sb("expert_no", [P, E])
        class_no = sb("class_no", [P, K])
        pair_of = sb("pair_of", [P, 2, K])
        part_no = sb("part_no", [P, 1])
        empty_row = sb("empty_row", [P, NS])
        ones_h = sb("ones_h", [P, P], BF16)
        before_h = sb("before_h", [P, P], BF16)
        wide = sb("wide", [P, 2 * K * NT])
        slot_w = wide[:, 0:K * NT].rearrange("p (k t) -> p k t", t=NT)
        member = wide[:, K * NT:3 * K * NT // 2].bitcast(BF16).rearrange("p (k t) -> p k t", t=NT)
        tile_before = wide[0:NT, 3 * K * NT // 2:2 * K * NT].bitcast(BF16).rearrange("p (k t) -> p k t", t=NT)
        tile_sum = sb("tile_sum", [NT, K], BF16)
        class_sum = sb("class_sum", [K, 1], I32)
        class_tiles = sb("class_tiles", [K, 1], I32)
        class_tilesf = sb("class_tilesf", [K, 1])
        bounds_r = sb("bounds_r", [K, 2, K])
        bounds = sb("bounds", [P, 2, K])
        bounds_w = sb("bounds_w", [P, K])
        slot = sb("slot", [P, NT])
        slot_u = sb("slot_u", [P, NT], U32)
        in_class = sb("in_class", [P, 2, K])
        is_class = sb("is_class", [P, K])
        pairs_w = sb("pairs_w", [P, 2, K])
        pairs = sb("pairs", [P, 2])
        pair_row = sb("pair_row", [1, P, 2], I32)
        zeros = sb("zeros", [P, ROW])

        xr = sb("xr", [P, G, D])
        th, sg, kg, ek, rk, eq, rq = (wide[:, a * GW:(a + 1) * GW] for a in range(7))
        kp = sb("kp", [P, 2, G, P])
        qp = sb("qp", [P, 2, G, P])
        v1 = sb("v1", [P, 2, G, D1])
        ktok = sb("ktok", [P, G, P])
        scores = sb("scores", [P, 2, G, P])
        state = sb("state", [P, C, D1])
        den = sb("den", [P, G])
        rden = sb("rden", [P, G])

        row = sb("row", [P, TILES, ROW])
        xT = sb("xT", [P, 2, P])
        y = sb("y", [P, TILES, D])
        e_tmp = sb("e_tmp", [P, TILES])
        y_row = sb("y_row", [P, TILES], U32)
        relu = sb("relu", [P, 2, FF])
        h = sb("h", [P, 2, FF])
        hT = sb("hT", [P, 2, FB, P])

        psum = ctx.enter_context(nc.psum_tensor("psum", [P, 8, 512], F32))

        x_in = [sem("x_in0"), sem("x_in1")]
        w_loaded = sem("w_loaded")
        ew_loaded = sem("ew_loaded")
        const_ready = sem("const_ready")
        prep_pe = sem("prep_pe")
        prep_dve = sem("prep_dve")
        stat_step = sem("stat_step")
        sqrt_out = sem("sqrt_out")
        route_dve = sem("route_dve")
        route_act = sem("route_act")
        route_pe = sem("route_pe")
        cleared = sem("cleared")
        scattered = sem("scattered")
        row_in = [sem(f"row_in{q}") for q in range(TILES)]
        y_out = [sem(f"y_out{q}") for q in range(TILES)]
        y_back = [sem(f"y_back{b}") for b in range(B)]
        y_going = sem("y_going")
        total = sem("total")
        stored = sem("stored")

        def steps(names):
            return [sem(name) for name in names.split()]

        pool_steps = z_kept, zT_kept, xr_done, base_ready = steps("z_kept zT_kept xr_done base_ready")
        act_steps = (zT_saved, th_done, ek_done, rq_done, kt_saved, s_saved, relu_done, hT_saved) = steps(
            "zT_saved th_done ek_done rq_done kt_saved s_saved relu_done hT_saved")
        dve_steps = (z_ready, logit_saved, za_ready, sg_done, kg_done, kp_done, qp_done, v_saved, a_masked, o_used,
                     rden_step, h_done, xT_ready, y_saved, row_step) = steps(
            "z_ready logit_saved za_ready sg_done kg_done kp_done qp_done v_saved a_masked o_used "
            "rden_step h_done xT_ready y_saved row_step")
        pe_steps = (zT_ready, logit_ready, g_ready, k_ready, q_ready, v_ready, a_ready, kt_ready, s_ready, o_ready,
                    row_turned, gu_ready, hT_ready, wo_done) = steps(
            "zT_ready logit_ready g_ready k_ready q_ready v_ready a_ready kt_ready s_ready o_ready "
            "row_turned gu_ready hT_ready wo_done")

        def start(eng, mine):
            for s in mine:
                eng.sem_inc(s, AHEAD)

        def wait(eng, s, count):
            if not isinstance(count, int) or count > 0:
                eng.wait_ge(s, count + AHEAD)

        def loop_and_last(eng, n, body):
            with eng.Fori(0, n - 1) as i:
                body(i, False)
            body(n - 1, True)

        WQ, WK, WV, WG = (slice(i * D, (i + 1) * D) for i in range(4))
        PAIRS = B // 2
        NCONST = 7 + 6 + 2 * (E - 1) + 3
        ROUND = 11
        ROW_SHIFTED, ROW_SUMMED, TOKEN_MAX, DIAG, COL_SHIFTED, COL_SUMMED = 2, 3, 5, 7, 9, 10

        def route_step(s, place=0):
            return 2 + ROUND * s + place

        MEMBER_STEP = route_step(SINKHORN_ITERS) + 4 + 11 + 1 + 6 + 14
        TILE_SUM_STEP = MEMBER_STEP + 1
        TILE_BEFORE_STEP = TILE_SUM_STEP + 1
        BOUNDS_STEP = TILE_BEFORE_STEP + 4
        SLOTS_STEP = BOUNDS_STEP + 6
        PAIRS_STEP = SLOTS_STEP + 4
        PAIR_ROW_STEP = PAIRS_STEP + 1
        ROUTE_PE_TILES = 3 * SINKHORN_ITERS + 1
        ROUTE_PE_CLASSES = ROUTE_PE_TILES + 1
        ROUTE_PE_BOUNDS = ROUTE_PE_CLASSES + 2
        ROUTE_PE_PAIRS = ROUTE_PE_BOUNDS + 1

        block = ctx.enter_context(nc.Block())

        @block.sync
        def _(sp):
            def load_x(b, j):
                sp.dma_start(xs[:, bass.ds(b * C, C), :], x_view[bass.ds(b, 1)]
                             .rearrange("a p c d -> p (a c) d")).then_inc(x_in[j], 16)

            load_x(0, 0)
            load_x(1, 1)
            with sp.Fori(1, PAIRS) as i:
                for j in range(2):
                    sp.wait_ge(x_in[j], 16 * i)
                    load_x(2 * i + j, j)
            sp.dma_start(w_gp[:, :, 0:FF], wg.rearrange("e d f -> d e f")).then_inc(ew_loaded, 16)
            sp.dma_start(w_gp[:, :, FF:2 * FF], wp.rearrange("e d f -> d e f")).then_inc(ew_loaded, 16)
            sp.dma_start(w_o[:, :, :, :], wo.rearrange("e (b p) d -> p e b d", p=P)).then_inc(ew_loaded, 16)
            sp.wait_ge(const_ready, NCONST)
            sp.dma_start(sorted_rows.rearrange("(n p) r -> p n r", p=P),
                         zeros[:].unsqueeze(1).to_broadcast([P, NS, ROW])).then_inc(cleared, 16)

            def load_row(m, q):
                i = m * TILES + q
                wait(sp, relu_done, 2 * (i - TILES + 1))
                wait(sp, row_step, 2 * (i - TILES + 1))
                sp.dma_start(row[:, q, :], sorted_rows.rearrange("(n p) r -> n p r", p=P)[bass.ds(i, 1)]
                             .rearrange("a p r -> p (a r)")).then_inc(row_in[q], 16)
            sp.wait_ge(scattered, 16 * NT)
            for q in range(TILES):
                load_row(0, q)
            with sp.Fori(1, NS // TILES) as m:
                for q in range(TILES):
                    load_row(m, q)

            for q in range(TILES):
                sp.wait_ge(y_out[q], 16 * (NS // TILES))
            for b in range(B):
                sp.dma_start(rows[:, b * C:(b + 1) * C, 0:D],
                             expert_out[b * T:(b + 1) * T, :].rearrange("(c p) d -> p c d", p=P))\
                  .then_inc(y_back[b], 16)

        @block.gpsimd
        def _(pool):
            start(pool, pool_steps)
            pool.memset(ones[:], 1.0).then_inc(const_ready, 1)
            pool.memset(ones_h[:], 1.0).then_inc(const_ready, 1)
            pool.memset(ident[:], 0.0).then_inc(const_ready, 1)
            pool.memset(causal[:], 1.0).then_inc(const_ready, 1)
            pool.memset(before_h[:], 1.0).then_inc(const_ready, 1)
            pool.memset(v1[:], 1.0).then_inc(const_ready, 1)
            pool.memset(zeros[:], 0.0).then_inc(const_ready, 1)

            def count_up(out, pattern, base, per_partition=0):
                pool.iota(out, pattern=pattern, base=base, channel_multiplier=per_partition,
                          allow_small_or_imprecise_dtypes=True).then_inc(const_ready, 1)

            count_up(rank[:], [[-1, E]], E)
            count_up(expert_no[:], [[1, E]], 0)
            count_up(class_no[:], [[1, K]], 0)
            count_up(part_no[:], [[1, 1]], 0, 1)
            count_up(empty_row[:], [[P, NS]], NTOK + 1, 1)
            count_up(rows[:, :, D + 2], [[P, NT]], 1, 1)
            first = 0
            for e in range(E - 1):
                count_up(pair_of[:, 0, first:first + E - 1 - e], [[0, E - 1 - e]], e)
                count_up(pair_of[:, 1, first:first + E - 1 - e], [[1, E - 1 - e]], e + 1)
                first += E - 1 - e
            pool.wait_ge(const_ready, NCONST - 3)
            pool.affine_select(out=ident[:], in_=ident[:], compare_op=ALU.not_equal, fill=1.0, base=0,
                               pattern=[[-1, P]], channel_multiplier=1).then_inc(const_ready, 1)
            pool.affine_select(out=causal[:], in_=causal[:], compare_op=ALU.is_ge, fill=0.0, base=0,
                               pattern=[[1, P]], channel_multiplier=-1).then_inc(const_ready, 1)
            pool.affine_select(out=before_h[:], in_=before_h[:], compare_op=ALU.is_ge, fill=0.0, base=-1,
                               pattern=[[1, P]], channel_multiplier=-1).then_inc(const_ready, 1)

            with pool.Fori(0, PAIRS) as i:
                for gl in range(2 * GB):
                    n = 2 * GB * i + gl
                    wait(pool, z_ready, n + 1)
                    pool.tensor_copy(rows[:, bass.ds(n * G, G), 0:D], z[:, gl % 2]).then_inc(z_kept, 1)
                    wait(pool, zT_saved, n + 1)
                    pool.tensor_copy(zT[:, bass.ds(n * G, G), :], zTg[:, gl % 2]).then_inc(zT_kept, 1)

            pool.wait_ge(prep_dve, 8)
            with pool.Fori(0, NG) as n:
                tiles = bass.ds(n * G, G)
                wait(pool, base_ready, n)
                pool.tensor_tensor(xr[:], xs[:, tiles, :], r1p[:, tiles].unsqueeze(2).to_broadcast([P, G, D]),
                                   ALU.mult).then_inc(xr_done, 1)
                wait(pool, xr_done, n + 1)
                pool.tensor_tensor(xs[:, tiles, :], xr[:], mr[:, tiles].unsqueeze(2).to_broadcast([P, G, D]),
                                   ALU.subtract).then_inc(base_ready, 1)

            pool.wait_ge(cleared, 16)
            wait(pool, z_kept, NG)
            pool.wait_ge(route_dve, SLOTS_STEP)
            for i in range(NT):
                pool.indirect_dma_start(sorted_rows, bass.IndirectOffsetOnAxis(ap=slot_u[:, i:i + 1], axis=0),
                                        rows[:, i, :], None).then_inc(scattered, 16)

            with pool.Fori(0, NS // TILES) as m:
                for q in range(TILES):
                    wait(pool, y_saved, m * TILES + q + 1)
                    pool.sem_inc(y_going, 1)
                    pool.indirect_dma_start(expert_out,
                                            bass.IndirectOffsetOnAxis(ap=y_row[:, q:q + 1], axis=0),
                                            y[:, q, :], None).then_inc(y_out[q], 16)

        @block.scalar
        def _(act):
            start(act, act_steps)
            act.dma_start(w_raw[:, 0:3 * D], qkv_w).then_inc(w_loaded, 16)
            act.dma_start(w_raw[:, WG], gate_w).then_inc(w_loaded, 16)
            act.dma_start(g_col[:], ln_g.rearrange("(p a) -> p a", a=1)).then_inc(w_loaded, 16)
            act.dma_start(b_col[:], ln_b.rearrange("(p a) -> p a", a=1)).then_inc(w_loaded, 16)
            act.dma_start(bias_in[:, 0:3], qkv_b.rearrange("(a p) -> p a", p=P), allow_slow_non_contiguous=True).then_inc(w_loaded, 16)
            act.dma_start(bias_in[:, 3:4], gate_b.rearrange("(p a) -> p a", a=1)).then_inc(w_loaded, 16)
            act.dma_start(bv_raw[:], qkv_b[2 * D:3 * D].partition_broadcast(P)).then_inc(w_loaded, 16)
            act.dma_start(rw_raw[:], router_w).then_inc(w_loaded, 16)
            act.dma_start(rb[:], router_b.partition_broadcast(P)).then_inc(w_loaded, 16)
            act.dma_start(temp[:], temperature.partition_broadcast(P)).then_inc(w_loaded, 16)

            act.wait_ge(stat_step, 6)
            act.activation(sq[:], va[:], ACT.Sqrt).then_inc(sqrt_out, 1)
            with act.Fori(0, PAIRS) as i:
                for gl in range(2 * GB):
                    n = 2 * GB * i + gl
                    wait(act, zT_ready, n + 1)
                    wait(act, zT_kept, n - 1)
                    wait(act, logit_ready, n - 1)
                    act.activation(zTg[:, gl % 2], psum[:, gl % 2, :].rearrange("p (g t) -> p g t", g=G),
                                   ACT.Copy).then_inc(zT_saved, 1)

            for s in range(SINKHORN_ITERS):
                act.wait_ge(route_dve, route_step(s, ROW_SHIFTED))
                act.activation(rB[:], rA[:], ACT.Exp).then_inc(route_act, 1)
                act.wait_ge(route_dve, route_step(s, ROW_SUMMED))
                act.activation(u64[:], t64[:], ACT.Ln).then_inc(route_act, 1)
                act.wait_ge(route_dve, route_step(s, COL_SHIFTED))
                act.activation(rB[:], rA[:], ACT.Exp).then_inc(route_act, 1)
                act.wait_ge(route_pe, 3 * s + 3)
                act.activation(u64[:], psum[:, 2, 0:NT], ACT.Ln).then_inc(route_act, 1)
            act.wait_ge(route_dve, route_step(SINKHORN_ITERS))
            act.activation(rB[:], rC[:], ACT.Exp).then_inc(route_act, 1)

            def tanh_gate(n):
                wait(act, g_ready, n + 1)
                wait(act, sg_done, n)
                act.activation(th, psum[:, 0, :], ACT.Tanh, bias=hbg[:], scale=0.5).then_inc(th_done, 1)

            def exp_query(n):
                wait(act, q_ready, n + 1)
                wait(act, qp_done, n)
                act.activation(eq, psum[:, 2, :], ACT.Exp, bias=bias_col[:, 0:1])
                act.activation(rq, psum[:, 2, :], ACT.Relu, bias=bias_col[:, 0:1]).then_inc(rq_done, 1)

            def exp_key(n):
                wait(act, kg_done, n + 1)
                wait(act, kp_done, n)
                act.activation(ek, kg, ACT.Exp)
                act.activation(rk, kg, ACT.Relu).then_inc(ek_done, 1)

            def copy_state(b, hb, c):
                cb = G * hb + c
                if cb == C - 1:
                    return
                wait(act, s_ready, (C - 1) * b + cb + 1)
                wait(act, o_ready, GB * b + hb - 1 + (1 if cb + 1 == G else 0))
                act.activation(state[:, cb + 1, :], psum[:, 5, 0:D1], ACT.Copy).then_inc(s_saved, 1)

            def batch(b, is_last):
                for hb in range(GB):
                    n = GB * b + hb
                    ahead = not (is_last and hb == GB - 1)
                    wait(act, kt_ready, n + 1)
                    wait(act, s_ready, (C - 1) * b + G * hb)
                    act.activation(ktok[:], psum[:, 3, :].rearrange("p (g t) -> p g t", g=G), ACT.Copy)\
                       .then_inc(kt_saved, 1)
                    copy_state(b, hb, 0)
                    if ahead:
                        tanh_gate(n + 1)
                    copy_state(b, hb, 1)
                    copy_state(b, hb, 2)
                    if ahead:
                        exp_query(n + 1)
                        exp_key(n + 1)
                    copy_state(b, hb, 3)

            act.wait_ge(prep_dve, 8)
            tanh_gate(0)
            exp_query(0)
            exp_key(0)
            loop_and_last(act, B, batch)

            def save_hT(k, kb):
                wait(act, hT_ready, k + 1)
                act.activation(hT[:, kb], psum[:, 2 + kb, 0:FF].rearrange("p (b t) -> p b t", b=FB),
                               ACT.Copy).then_inc(hT_saved, 1)

            def expert(m, q, e):
                k = 2 * (m * TILES + q) + e
                wait(act, gu_ready, k + 1)
                act.activation(relu[:, e, :], psum[:, e, 0:FF], ACT.Relu,
                               scale=row[:, q, D + e:D + e + 1]).then_inc(relu_done, 1)
                if not (isinstance(k, int) and k == 0):
                    save_hT(k - 1, 1 - e)

            def four_tiles(m):
                for q in range(TILES):
                    for e in range(2):
                        expert(m, q, e)

            four_tiles(0)
            with act.Fori(1, NS // TILES) as m:
                four_tiles(m)
            save_hT(2 * NS - 1, 1)

            for b in range(B):
                act.wait_ge(total, b + 1)
                act.dma_start(out_view[b], xs[:, b * C:(b + 1) * C, :]).then_inc(stored, 16)
            act.wait_ge(stored, 16 * B)

        @block.vector
        def _(dve):
            start(dve, dve_steps)
            dve.wait_ge(w_loaded, 16 * 10)
            dve.wait_ge(const_ready, NCONST)
            dve.tensor_scalar(w_in[:, WQ], w_raw[:, WQ], g_col[:], None, ALU.mult)
            dve.tensor_scalar(w_in[:, 2 * D:4 * D], w_raw[:, 2 * D:4 * D], g_col[:], None, ALU.mult)\
               .then_inc(prep_dve, 1)
            dve.tensor_scalar(b_wide[:], ones[:], b_col[:], None, ALU.mult)
            dve.tensor_scalar(w_in[:, WK], w_raw[:, WK], g_col[:], 0.5, ALU.mult, ALU.mult).then_inc(prep_dve, 1)
            dve.wait_ge(prep_pe, 1)
            dve.tensor_tensor(bias_col[:], psum[:, 0, 0:4], bias_in[:], ALU.add).then_inc(prep_dve, 1)
            dve.tensor_tensor(bv[:], psum[:, 1, 0:D], bv_raw[:], ALU.add)
            dve.tensor_copy(rwT[:], psum[:, 2, 0:E])
            dve.tensor_scalar(temp_c[:], temp[:], TEMP_MIN, None, ALU.max).then_inc(prep_dve, 1)
            dve.wait_ge(prep_dve, 4)
            dve.tensor_scalar(hbg[:], bias_col[:, 3:4], 0.5, None, ALU.mult)
            dve.tensor_scalar(hbk[:], bias_col[:, 1:2], 0.5, None, ALU.mult)
            dve.reciprocal(rtemp[:], temp_c[:]).then_inc(prep_dve, 1)

            with dve.Fori(0, PAIRS) as i:
                for j in range(2):
                    dve.wait_ge(x_in[j], 16 * (i + 1))
                    for c in range(C):
                        ti = (2 * i + j) * C + c
                        last = dve.bn_stats(stats[:, bass.ds(ti, 1), :].rearrange("p a d -> p (a d)"),
                                            xs[:, bass.ds(ti, 1), :].rearrange("p a d -> p (a d)"))
            stat = [0]

            def stat_link(*these):
                stat[0] += 1
                these[-1].then_inc(stat_step, 1)
                dve.wait_ge(stat_step, stat[0])

            stat_link(dve.engine_nop())
            stat_link(dve.tensor_tensor(m_sum[:], stats[:, :, 1], stats[:, :, 4], ALU.add),
                      dve.tensor_tensor(m_dif[:], stats[:, :, 1], stats[:, :, 4], ALU.subtract),
                      dve.tensor_tensor(m_sq[:], stats[:, :, 2], stats[:, :, 5], ALU.add))
            stat_link(dve.scalar_tensor_tensor(m_dif2[:], m_dif[:], 0.25, m_dif[:], ALU.mult, ALU.mult),
                      dve.tensor_scalar(mean[:], m_sum[:], 0.5, None, ALU.mult))
            stat_link(dve.scalar_tensor_tensor(var[:], m_sq[:], 1.0 / D, m_dif2[:], ALU.mult, ALU.add))
            stat_link(dve.tensor_scalar(va[:, 0, :], var[:], LN_EPS, None, ALU.add))
            dve.reciprocal(ra[:], va[:, 0, :]).then_inc(prep_dve, 1)
            dve.wait_ge(prep_dve, 6)
            dve.tensor_tensor(v2[:], var[:], ra[:], ALU.mult).then_inc(prep_dve, 1)
            dve.wait_ge(prep_dve, 7)
            stat_link(dve.tensor_scalar(va[:, 1, :], v2[:], LN_EPS, None, ALU.add))
            dve.wait_ge(sqrt_out, 1)
            stat_link(dve.reciprocal(rs[:], sq[:]))
            stat_link(dve.tensor_tensor(r12[:], rs[:, 0, :], rs[:, 1, :], ALU.mult))
            dve.tensor_tensor(mr[:], mean[:], rs[:, 0, :], ALU.mult)
            dve.tensor_scalar(r1p[:], rs[:, 0, :], 1.0, None, ALU.add).then_inc(prep_dve, 1)

            def save_logits(b, j):
                wait(dve, logit_ready, GB * (b + 1))
                tiles = bass.ds(b * C, C)
                dve.tensor_tensor(gate[:, tiles, :], psum[:, 2 + j, 0:C * E].rearrange("p (c e) -> p c e", e=E),
                                  sq[:, 1, tiles].unsqueeze(2).to_broadcast([P, C, E]), ALU.mult)\
                   .then_inc(logit_saved, 1)

            def normalise(n, hb):
                wait(dve, zT_ready, n - 1)
                wait(dve, z_kept, n - 1)
                for t in range(G):
                    ti = n * G + t
                    last = dve.tensor_scalar(z[:, hb, t, :], xs[:, bass.ds(ti, 1), :].rearrange("p a d -> p (a d)"),
                                             mean[:, bass.ds(ti, 1)], r12[:, bass.ds(ti, 1)],
                                             ALU.subtract, ALU.mult)
                last.then_inc(z_ready, 1)

            def pair_of_batches(i, first):
                for j in range(2):
                    normalise(2 * GB * i + GB * j, 0)
                    normalise(2 * GB * i + GB * j + 1, 1)
                    if not (first and j == 0):
                        save_logits(2 * i + j - 1, 1 - j)
            pair_of_batches(0, True)
            with dve.Fori(1, PAIRS) as i:
                pair_of_batches(i, False)
            save_logits(B - 1, 1)

            chain = [0]

            def link(ins):
                chain[0] += 1
                ins.then_inc(route_dve, 1)
                dve.wait_ge(route_dve, chain[0])

            def over_e(a):
                return a.unsqueeze(2).to_broadcast([P, NT, E])

            def by_batch(a):
                return a.rearrange("p (b c) e -> p b c e", c=C)

            def over_c(a):
                return a.rearrange("p (b e) -> p b e", e=E).unsqueeze(2).to_broadcast([P, B, C, E])

            wait(dve, logit_saved, B)
            link(dve.tensor_tensor(rA[:], gate[:], rb[:].unsqueeze(1).to_broadcast([P, NT, E]), ALU.add))
            link(dve.tensor_scalar(rC[:], rA[:], rtemp[:], None, ALU.mult))
            acts = 0
            for s in range(SINKHORN_ITERS):
                link(dve.tensor_reduce(t64[:], rC[:], AX_X, ALU.max))
                link(dve.tensor_tensor(rA[:], rC[:], over_e(t64[:]), ALU.subtract))
                acts += 1
                dve.wait_ge(route_act, acts)
                link(dve.tensor_reduce(t64[:], rB[:], AX_X, ALU.add))
                acts += 1
                dve.wait_ge(route_act, acts)
                link(dve.tensor_tensor(rC[:], rA[:], over_e(u64[:]), ALU.subtract))
                link(dve.tensor_reduce(t64[:].rearrange("p (b e) -> p b e", e=E),
                                       by_batch(rC[:]).rearrange("p b c e -> p b e c"), AX_X, ALU.max))
                dve.wait_ge(route_pe, 3 * s + 1)
                link(dve.tensor_reduce(cmax[:], psum[0:NT, 0, 0:P], AX_X, ALU.max))
                link(dve.tensor_scalar(diag[:], ident[0:NT, 0:NT], cmax[:], None, ALU.mult))
                dve.wait_ge(route_pe, 3 * s + 2)
                link(dve.tensor_copy(v64[:], psum[:, 1, 0:NT]))
                link(dve.tensor_tensor(by_batch(rA[:]), by_batch(rC[:]), over_c(v64[:]), ALU.subtract))
                acts += 1
                dve.wait_ge(route_act, acts)
                link(dve.tensor_reduce(t64[:].rearrange("p (b e) -> p b e", e=E),
                                       by_batch(rB[:]).rearrange("p b c e -> p b e c"), AX_X, ALU.add))
                acts += 1
                dve.wait_ge(route_act, acts)
                link(dve.tensor_tensor(by_batch(rC[:]), by_batch(rA[:]), over_c(u64[:]), ALU.subtract))
                assert chain[0] == route_step(s + 1)
            acts += 1
            dve.wait_ge(route_act, acts)
            link(dve.tensor_reduce(t64[:], rB[:], AX_X, ALU.add))
            link(dve.tensor_scalar(u64[:], t64[:], GATE_EPS, None, ALU.add))
            link(dve.reciprocal(v64[:], u64[:]))
            link(dve.tensor_tensor(gate[:], rB[:], over_e(v64[:]), ALU.mult))
            ranks = rank[:].unsqueeze(1).to_broadcast([P, NT, E])

            def top(src, vmax, onehot):
                link(dve.tensor_reduce(vmax, src, AX_X, ALU.max))
                link(dve.tensor_tensor(rB[:], src, over_e(vmax), ALU.is_ge))
                link(dve.tensor_tensor(rB[:], rB[:], ranks, ALU.mult))
                link(dve.tensor_reduce(v64[:], rB[:], AX_X, ALU.max))
                link(dve.tensor_tensor(onehot, rB[:], over_e(v64[:]), ALU.is_equal))

            top(gate[:], t64[:], rA[:])
            link(dve.scalar_tensor_tensor(rC[:].rearrange("p t e -> p (t e)"), rA[:].rearrange("p t e -> p (t e)"),
                                          -BIG, gate[:].rearrange("p t e -> p (t e)"), ALU.mult, ALU.add))
            top(rC[:], u64[:], rC[:])
            link(dve.tensor_tensor(rA[:], rA[:], rC[:], ALU.add))
            link(dve.tensor_tensor(t64[:], t64[:], u64[:], ALU.add))
            link(dve.tensor_scalar(t64[:], t64[:], GATE_EPS, None, ALU.add))
            link(dve.reciprocal(u64[:], t64[:]))
            link(dve.tensor_tensor(u64[:], u64[:], sq[:, 1, :], ALU.mult))
            link(dve.tensor_tensor(u64[:], u64[:], sq[:, 1, :], ALU.mult))
            link(dve.tensor_tensor(gate[:], gate[:], over_e(u64[:]), ALU.mult))

            numbers = expert_no[:].unsqueeze(1).to_broadcast([P, NT, E])
            link(dve.tensor_tensor(rB[:], rA[:], ranks, ALU.mult))
            link(dve.tensor_reduce(t64[:], rB[:], AX_X, ALU.max))
            link(dve.tensor_tensor(rC[:], rB[:], over_e(t64[:]), ALU.is_equal))
            link(dve.tensor_tensor(rB[:], rC[:], gate[:], ALU.mult))
            link(dve.tensor_reduce(rows[:, :, D], rB[:], AX_X, ALU.add))
            link(dve.tensor_tensor(rB[:], rA[:], numbers, ALU.mult))
            link(dve.tensor_reduce(u64[:], rB[:], AX_X, ALU.max))
            link(dve.tensor_tensor(rC[:], rB[:], over_e(u64[:]), ALU.is_equal))
            link(dve.tensor_tensor(rB[:], rC[:], gate[:], ALU.mult))
            link(dve.tensor_reduce(rows[:, :, D + 1], rB[:], AX_X, ALU.add))
            link(dve.tensor_scalar(v64[:], t64[:], -0.5, 1.5, ALU.mult, ALU.add))
            link(dve.tensor_tensor(v64[:], v64[:], t64[:], ALU.mult))
            link(dve.scalar_tensor_tensor(v64[:], v64[:], float(K - E - 1), u64[:], ALU.add, ALU.add))
            link(dve.tensor_tensor(member, v64[:].unsqueeze(1).to_broadcast([P, K, NT]),
                                   class_no[:].unsqueeze(2).to_broadcast([P, K, NT]), ALU.is_equal))
            assert chain[0] == MEMBER_STEP
            dve.wait_ge(route_pe, ROUTE_PE_TILES)
            link(dve.tensor_copy(tile_sum[:], psum[0:NT, 0, 0:K]))
            assert chain[0] == TILE_SUM_STEP
            link(dve.tensor_tensor(tile_before, tile_sum[:].unsqueeze(2).to_broadcast([NT, K, NT]),
                                   before_h[0:NT, 0:NT].unsqueeze(1).to_broadcast([NT, K, NT]), ALU.mult))
            assert chain[0] == TILE_BEFORE_STEP
            dve.wait_ge(route_pe, ROUTE_PE_CLASSES)
            link(dve.tensor_scalar(class_sum[:], psum[0:K, 1, 0:1], float(P - 1), None, ALU.add))
            link(dve.tensor_scalar(class_tiles[:], class_sum[:], P.bit_length() - 1, None, ALU.arith_shift_right))
            link(dve.tensor_copy(class_tilesf[:], class_tiles[:]))
            dve.tensor_scalar(bounds_r[:, 1, :], causal[0:K, 0:K], class_tilesf[:], None, ALU.mult)
            link(dve.tensor_scalar(bounds_r[:, 0, :], before_h[0:K, 0:K], class_tilesf[:], None, ALU.mult))
            assert chain[0] == BOUNDS_STEP
            dve.wait_ge(route_pe, ROUTE_PE_BOUNDS)
            link(dve.tensor_copy(bounds[:].rearrange("p a k -> p (a k)"), psum[:, 2, 0:2 * K]))
            link(dve.tensor_scalar(bounds_w[:], bounds[:, 0, :], float(P), None, ALU.mult))
            for g in range(K // KB):
                classes = slice(g * KB, (g + 1) * KB)
                last = dve.tensor_tensor(slot_w[:, classes, :],
                                         psum[:, 4 + g, 0:KB * NT].rearrange("p (k t) -> p k t", t=NT),
                                         bounds_w[:, classes].unsqueeze(2).to_broadcast([P, KB, NT]), ALU.add)
            link(last)
            link(dve.tensor_tensor(slot_w, slot_w, member, ALU.mult))
            link(dve.tensor_reduce(slot[:], slot_w.rearrange("p k t -> p t k"), AX_X, ALU.add))
            link(dve.tensor_copy(slot_u[:], slot[:]))
            assert chain[0] == SLOTS_STEP
            link(dve.tensor_scalar(in_class[:], bounds[:], part_no[:], None, ALU.is_le))
            link(dve.tensor_tensor(is_class[:], in_class[:, 0, :], in_class[:, 1, :], ALU.subtract))
            link(dve.tensor_tensor(pairs_w[:], pair_of[:], is_class[:].unsqueeze(1).to_broadcast([P, 2, K]),
                                   ALU.mult))
            link(dve.tensor_reduce(pairs[:], pairs_w[:], AX_X, ALU.add))
            assert chain[0] == PAIRS_STEP
            dve.wait_ge(route_pe, ROUTE_PE_PAIRS)
            link(dve.tensor_copy(pair_row[:].rearrange("o t a -> o a t"),
                                 psum[0:1, 3, 0:2 * P].rearrange("o (a t) -> o a t", a=2)))
            assert chain[0] == PAIR_ROW_STEP

            def finish(n):
                wait(dve, o_ready, n + 1)
                for j in range(2):
                    o2 = psum[:, 6 + j, 0:2 * D1].rearrange("p (k x) -> p k x", x=D1)
                    last = dve.tensor_scalar(den[:, 2 * j:2 * j + 2].unsqueeze(2), o2[:, :, D:D1], DEN_EPS, None,
                                             ALU.add)
                last.then_inc(rden_step, 1)
                wait(dve, rden_step, 2 * n + 1)
                dve.reciprocal(rden[:], den[:]).then_inc(rden_step, 1)
                wait(dve, rden_step, 2 * n + 2)
                wait(dve, base_ready, n + 1)
                for t in range(G):
                    o = psum[:, 6 + t // 2, (t % 2) * D1:(t % 2) * D1 + D]
                    acc = xs[:, bass.ds(n * G + t, 1), :].rearrange("p a d -> p (a d)")
                    last = dve.scalar_tensor_tensor(acc, o, rden[:, t:t + 1], acc, ALU.mult, ALU.add)
                last.then_inc(o_used, 1)

            def fetch_zT(n, hb):
                wait(dve, v_ready, n - 1)
                dve.tensor_copy(zTg[:, hb], zT[:, bass.ds(n * G, G), :]).then_inc(za_ready, 1)

            def group(n, hb, is_last=False):
                wait(dve, th_done, n + 1)
                dve.tensor_scalar(sg, th, 1.0, None, ALU.add).then_inc(sg_done, 1)
                wait(dve, k_ready, n + 1)
                wait(dve, sg_done, n + 1)
                wait(dve, ek_done, n)
                dve.scalar_tensor_tensor(kg, psum[:, 1, :], hbk[:], sg, ALU.add, ALU.mult)\
                   .then_inc(kg_done, 1)
                wait(dve, rq_done, n + 1)
                if not is_last:
                    fetch_zT(n + 1, 1 - hb)
                wait(dve, o_ready, n - 1)
                dve.scalar_tensor_tensor(qp[:, hb].rearrange("p g t -> p (g t)"), eq, 1.0, rq,
                                         ALU.min, ALU.add).then_inc(qp_done, 1)
                wait(dve, ek_done, n + 1)
                dve.scalar_tensor_tensor(kp[:, hb].rearrange("p g t -> p (g t)"), ek, 1.0, rk,
                                         ALU.min, ALU.add).then_inc(kp_done, 1)
                wait(dve, v_ready, n + 1)
                dve.tensor_tensor(v1[:, hb, :, 0:D], psum[:, 3, :].rearrange("p (g d) -> p g d", g=G),
                                  bv[:].unsqueeze(1).to_broadcast([P, G, D]), ALU.add).then_inc(v_saved, 1)

            def mask(n, hb):
                wait(dve, a_ready, n + 1)
                dve.tensor_tensor(scores[:, hb], psum[:, 4, :].rearrange("p (g t) -> p g t", g=G),
                                  causal[:].unsqueeze(1).to_broadcast([P, G, P]), ALU.mult).then_inc(a_masked, 1)

            wait(dve, zT_kept, NG)
            wait(dve, logit_ready, NG)
            fetch_zT(0, 0)
            group(0, 0)
            mask(0, 0)
            group(1, 1)
            finish(0)
            mask(1, 1)

            def batch(b, is_last):
                for hb in range(GB):
                    n = GB * b + hb
                    group(n, hb, is_last and hb == GB - 1)
                    finish(n - 1)
                    mask(n, hb)
            with dve.Fori(1, B - 1) as b:
                batch(b, False)
            batch(B - 1, True)
            finish(NG - 1)

            def save_xT(i, j):
                wait(dve, row_turned, i + 1)
                dve.tensor_copy(xT[:, j, :], psum[:, 6, 0:P]).then_inc(xT_ready, 1)

            def product(k, e):
                wait(dve, relu_done, k + 1)
                dve.tensor_tensor(h[:, e, :], relu[:, e, :], psum[:, e, FF:2 * FF], ALU.mult).then_inc(h_done, 1)

            def row_numbers(m, q):
                i = m * TILES + q
                dve.wait_ge(row_in[q], 16 * (m + 1))
                if not (isinstance(m, int) and m == 0):
                    dve.wait_ge(y_out[q], 16 * m)
                number = row[:, q, D + 2:D + 3]
                dve.tensor_scalar(e_tmp[:, q:q + 1], number, 0.0, empty_row[:, bass.ds(i, 1)], ALU.is_equal, ALU.mult)\
                   .then_inc(row_step, 1)
                wait(dve, row_step, 2 * i + 1)
                dve.scalar_tensor_tensor(y_row[:, q:q + 1], e_tmp[:, q:q + 1], -1.0, number, ALU.add, ALU.add)\
                   .then_inc(row_step, 1)

            def save_y(i, q):
                wait(dve, wo_done, 2 * (i + 1))
                dve.tensor_copy(y[:, q, :], psum[:, 4 + q % 2, 0:D]).then_inc(y_saved, 1)

            def four_tiles(m, is_first, is_last):
                for q in range(TILES):
                    i = m * TILES + q
                    product(2 * i, 0)
                    row_numbers(m, q)
                    product(2 * i + 1, 1)
                    if not (is_first and q == 0):
                        save_y(i - 1, (q - 1) % TILES)
                    if not (is_last and q >= TILES - 2):
                        save_xT(i + 2, q % 2)
            wait(dve, o_used, NG)
            save_xT(0, 0)
            save_xT(1, 1)
            four_tiles(0, True, False)
            with dve.Fori(1, NS // TILES - 1) as m:
                four_tiles(m, False, False)
            four_tiles(NS // TILES - 1, False, True)
            save_y(NS - 1, TILES - 1)

            for b in range(B):
                dve.wait_ge(y_back[b], 16)
                tiles = slice(b * C, (b + 1) * C)
                dve.tensor_tensor(xs[:, tiles, :], xs[:, tiles, :], rows[:, tiles, 0:D], ALU.add).then_inc(total, 1)

        @block.tensor
        def _(pe):
            start(pe, pe_steps)
            pe.wait_ge(w_loaded, 16 * 10)
            pe.wait_ge(const_ready, NCONST)
            pe.wait_ge(prep_dve, 2)
            for f in range(4):
                pe.matmul(psum[:, 0, f:f + 1], w_raw[:, f * D:(f + 1) * D], b_col[:], start=True, stop=True)
            pe.matmul(psum[:, 1, 0:D], b_wide[:], w_raw[:, WV], start=True, stop=True)
            pe.transpose(psum[:, 2, 0:E], rw_raw[:], ident[0:E, 0:E]).then_inc(prep_pe, 1)
            pe.wait_ge(prep_dve, 4)

            def turn_z(n, hb):
                wait(pe, z_ready, n + 1)
                wait(pe, zT_saved, n - 1)
                for t in range(G):
                    last = pe.transpose(psum[:, hb, t * P:(t + 1) * P], z[:, hb, t, :], ident[:])
                last.then_inc(zT_ready, 1)

            def score(b, j, hb):
                n = GB * b + hb
                wait(pe, zT_saved, n + 1)
                if hb == 0:
                    wait(pe, logit_saved, b - 1)
                for t in range(G):
                    c = G * hb + t
                    last = pe.matmul(psum[:, 2 + j, c * E:(c + 1) * E], zTg[:, hb, t, :], rwT[:],
                                     start=True, stop=True)
                last.then_inc(logit_ready, 1)

            def pair_of_batches(i, is_last):
                for j in range(2):
                    for hb in range(GB):
                        n = GB * (2 * i + j) + hb
                        if not (is_last and j == 1 and hb == GB - 1):
                            turn_z(n + 1, 1 - hb)
                        score(2 * i + j, j, hb)
            turn_z(0, 0)
            loop_and_last(pe, PAIRS, pair_of_batches)

            for s in range(SINKHORN_ITERS):
                pe.wait_ge(route_dve, route_step(s, TOKEN_MAX))
                pe.transpose(psum[0:NT, 0, 0:P], t64[:], ident[:]).then_inc(route_pe, 1)
                pe.wait_ge(route_dve, route_step(s, DIAG))
                pe.matmul(psum[:, 1, 0:NT], ones[0:NT, :], diag[:], start=True, stop=True).then_inc(route_pe, 1)
                pe.wait_ge(route_dve, route_step(s, COL_SUMMED))
                pe.matmul(psum[:, 2, 0:NT], ones[:], t64[:], start=True, stop=True).then_inc(route_pe, 1)
            pe.wait_ge(route_act, 4 * SINKHORN_ITERS)
            pe.wait_ge(route_dve, MEMBER_STEP)
            for k in range(K):
                last = pe.matmul(psum[0:NT, 0, k:k + 1], member[:, k, :], ones_h[:, 0:1], start=True, stop=True)
            last.then_inc(route_pe, 1)
            pe.wait_ge(route_dve, TILE_SUM_STEP)
            pe.matmul(psum[0:K, 1, 0:1], tile_sum[:], ones_h[0:NT, 0:1], start=True, stop=True).then_inc(route_pe, 1)
            pe.wait_ge(route_dve, TILE_BEFORE_STEP)
            for g in range(K // KB):
                classes = slice(g * KB, (g + 1) * KB)
                place = psum[:, 4 + g, 0:KB * NT]
                pe.matmul(place, before_h[:], member[:, classes, :].rearrange("p k t -> p (k t)"),
                          start=True, stop=False)
                last = pe.matmul(place, ones_h[0:NT, :], tile_before[:, classes, :].rearrange("p k t -> p (k t)"),
                                 start=False, stop=True)
            last.then_inc(route_pe, 1)
            pe.wait_ge(route_dve, BOUNDS_STEP)
            pe.matmul(psum[:, 2, 0:2 * K], ones[0:K, :], bounds_r[:].rearrange("p a k -> p (a k)"),
                      start=True, stop=True).then_inc(route_pe, 1)
            pe.wait_ge(route_dve, PAIRS_STEP)
            for a in range(2):
                last = pe.matmul(psum[0:1, 3, a * P:(a + 1) * P], pairs[:, a:a + 1], ident[:], start=True, stop=True)
            last.then_inc(route_pe, 1)
            pe.wait_ge(route_dve, PAIR_ROW_STEP)

            def project(n, hb, what):
                zt = zTg[:, hb].rearrange("p g t -> p (g t)")
                if what == "g":
                    wait(pe, za_ready, n + 1)
                    wait(pe, th_done, n)
                    pe.matmul(psum[:, 0, :], w_in[:, WG], zt, start=True, stop=True).then_inc(g_ready, 1)
                if what == "k":
                    wait(pe, kg_done, n)
                    pe.matmul(psum[:, 1, :], w_in[:, WK], zt, start=True, stop=True).then_inc(k_ready, 1)
                if what == "q":
                    wait(pe, rq_done, n)
                    pe.matmul(psum[:, 2, :], w_in[:, WQ], zt, start=True, stop=True).then_inc(q_ready, 1)
                if what == "v":
                    wait(pe, kt_saved, n)
                    for t in range(G):
                        last = pe.matmul(psum[:, 3, t * D:(t + 1) * D], zTg[:, hb, t, :], w_in[:, WV],
                                         start=True, stop=True)
                    last.then_inc(v_ready, 1)

            def group(b, hb, last_group):
                n = GB * b + hb
                wait(pe, kp_done, n + 1)
                wait(pe, qp_done, n + 1)
                wait(pe, a_masked, n)
                for c in range(G):
                    last = pe.matmul(psum[:, 4, c * P:(c + 1) * P], kp[:, hb, c, :], qp[:, hb, c, :],
                                     start=True, stop=True)
                last.then_inc(a_ready, 1)
                wait(pe, v_saved, n + 1)
                for c in range(G):
                    last = pe.transpose(psum[:, 3, c * P:(c + 1) * P], kp[:, hb, c, :], ident[:])
                last.then_inc(kt_ready, 1)
                for c, what in enumerate("gkqv"):
                    cb = G * hb + c
                    if not last_group:
                        project(n + 1, 1 - hb, what)
                    if c == 0:
                        wait(pe, kt_saved, n + 1)
                    if cb < C - 1:
                        wait(pe, s_saved, (C - 1) * b + cb)
                        pe.matmul(psum[:, 5, 0:D1], ktok[:, c, :], v1[:, hb, c, :],
                                  start=(cb == 0), stop=True, skip_group_check=True).then_inc(s_ready, 1)
                wait(pe, a_masked, n + 1)
                wait(pe, o_used, n)
                for c in range(G):
                    cb = G * hb + c
                    o = psum[:, 6 + c // 2, (c % 2) * D1:(c % 2 + 1) * D1]
                    last = pe.matmul(o, scores[:, hb, c, :], v1[:, hb, c, :], start=True, stop=(cb == 0))
                    if cb > 0:
                        wait(pe, s_saved, (C - 1) * b + cb)
                        last = pe.matmul(o, qp[:, hb, c, :], state[:, cb, :], start=False, stop=True)
                last.then_inc(o_ready, 1)

            for what in "gkqv":
                project(0, 0, what)

            def batch(b, is_last):
                for hb in range(GB):
                    group(b, hb, is_last and hb == GB - 1)
            loop_and_last(pe, B, batch)

            def turn_row(m, q):
                pe.wait_ge(row_in[q], 16 * (m + 1))
                pe.transpose(psum[:, 6, 0:P], row[:, q, 0:D], ident[:]).then_inc(row_turned, 1)

            def experts_of(i, tiles):
                _, numbers = nc.values_load_multi_w_load_instructions(
                    pair_row[:].rearrange("o t a -> o (t a)")[:, bass.ds(2 * i, 2 * tiles)],
                    engines=[mybir.EngineType.PE], min_val=0, max_val=E - 1, bass_reorder=False,
                    skip_runtime_bounds_check_because="a sum of at most one of pair_of's entries, all below E")
                return numbers

            def up(i, e, j, number):
                if e == 0:
                    wait(pe, xT_ready, i + 1)
                weights = w_gp[:, bass.ds(number, 1), :].rearrange("p a f -> p (a f)")
                pe.matmul(psum[:, e, :], xT[:, j, :], weights, start=True, stop=True).then_inc(gu_ready, 1)

            def turn(k, e):
                wait(pe, h_done, k + 1)
                for f in range(FB):
                    last = pe.transpose(psum[:, 2 + e, f * P:(f + 1) * P], h[:, e, f * P:(f + 1) * P], ident[:])
                last.then_inc(hT_ready, 1)

            def down(i, e, j, number):
                wait(pe, hT_saved, 2 * i + e + 1)
                if e == 0:
                    wait(pe, y_saved, i - 1)
                for f in range(FB):
                    weights = w_o[:, bass.ds(number, 1), f, :].rearrange("p a d -> p (a d)")
                    last = pe.matmul(psum[:, 4 + j, 0:D], hT[:, e, f, :], weights,
                                     start=(e == 0 and f == 0), stop=(e == 1 and f == FB - 1))
                last.then_inc(wo_done, 1)

            def four_tiles(m, is_last):
                numbers = experts_of(m * TILES, TILES + 1)
                for q in range(TILES):
                    for e in range(2):
                        i = m * TILES + q
                        ends = is_last and q == TILES - 1
                        if not ends:
                            up(i + 1, e, (q + 1) % 2, numbers[2 * (q + 1) + e])
                        if not (ends and e == 1):
                            turn(2 * i + e + 1, 1 - e)
                        down(i, e, q % 2, numbers[2 * q + e])
                        if e == 0 and not (is_last and q >= TILES - 2):
                            turn_row(m + (q + 2) // TILES, (q + 2) % TILES)
            pe.wait_ge(ew_loaded, 48)
            wait(pe, o_used, NG)
            first = experts_of(0, 1)
            turn_row(0, 0)
            wait(pe, xT_ready, 1)
            turn_row(0, 1)
            up(0, 0, 0, first[0])
            up(0, 1, 0, first[1])
            turn(0, 0)
            loop_and_last(pe, NS // TILES, four_tiles)


_INS = ["L0_attn_x", "L0_attn_qkv_w", "L0_attn_qkv_b", "L0_attn_gate_w", "L0_attn_gate_b", "L0_attn_ln_g",
        "L0_attn_ln_b", "L0_ffn_router_w", "L0_ffn_router_b", "L0_ffn_temperature", "L0_ffn_wg", "L0_ffn_wp",
        "L0_ffn_wo"]


def kernel(**inputs):
    import numpy as np
    import concourse.bacc as bacc
    from concourse.bass_utils import run_bass_kernel_spmd

    nc = bacc.Bacc("TRN2", target_bir_lowering=False, num_devices=1)
    arrays, args = {}, []
    for name in _INS:
        a = np.ascontiguousarray(inputs[name])
        arrays["in_" + name] = a
        args.append(nc.dram_tensor("in_" + name, a.shape, mybir.dt.from_np(a.dtype), kind="ExternalInput").ap())
    shape = arrays["in_L0_attn_x"].shape
    out = nc.dram_tensor("out", shape, F32, kind="ExternalOutput").ap()
    sparse_block_kernel(nc, *args, out)
    r = run_bass_kernel_spmd(nc, [arrays], core_ids=[0])
    return r.results[0]["out"]
```

```python
from contextlib import ExitStack

import concourse.bass as bass
from concourse import mybir

F32 = mybir.dt.float32
F32R = mybir.dt.float32r
BF16 = mybir.dt.bfloat16
I32 = mybir.dt.int32
U32 = mybir.dt.uint32
ALU = mybir.AluOpType
ACT = mybir.ActivationFunctionType
AX_X = mybir.AxisListType.X

LN_EPS = 1e-5
DEN_EPS = 1e-6
GATE_EPS = 1e-8
SINKHORN_ITERS = 3
TEMP_MIN = 0.1
BIG = 4.0
AHEAD = 4


def sparse_block_kernel(nc, x, qkv_w, qkv_b, gate_w, gate_b, ln_g, ln_b,
                        router_w, router_b, temperature, wg, wp, wo, out):
    P = nc.NUM_PARTITIONS
    B, T, D = x.shape
    E, _, FF = wg.shape
    C = T // P
    NT = B * C
    G = 4
    GW = G * P
    NG = NT // G
    GB = C // G
    D1 = D + 1
    FB = FF // P
    NTOK = NT * P
    K = E * (E - 1) // 2
    TILES = 4
    NS = -(-(NT + K - 1) // TILES) * TILES
    ROW = D + 3
    KB = 7
    assert D == P and C == 8 and GB == 2 and FB == 2 and K % KB == 0 and KB * NT <= 512 and NS <= P

    x_view = x.rearrange("b (c p) d -> b p c d", p=P)
    out_rows = out.rearrange("b t d -> (b t) d")
    sorted_rows = nc.dram_tensor("sorted_rows", (NS * P, ROW), F32).ap()
    base_rows = nc.dram_tensor("base_rows", (NTOK, D), F32).ap()

    with ExitStack() as ctx:
        def sb(name, shape, dt=F32):
            return ctx.enter_context(nc.sbuf_tensor(name, shape, dt))

        def sem(name):
            return ctx.enter_context(nc.semaphore(name))

        xs = sb("xs", [P, NT, D])
        zT = sb("zT", [P, NT, P])
        ident = sb("ident", [P, P])
        ones = sb("ones", [P, P])
        causal = sb("causal", [P, P])
        mean = sb("mean", [P, NT])
        rstd1 = sb("rstd1", [P, NT])
        std2 = sb("std2", [P, NT])
        var = sb("var", [P, NT])
        mr = sb("mr", [P, NT])
        r1p = sb("r1p", [P, NT])
        gate = sb("gate", [P, NT, E])

        w_raw = sb("w_raw", [P, 4 * D])
        w_in = sb("w_in", [P, 4 * D])
        g_col = sb("g_col", [P, 1])
        b_col = sb("b_col", [P, 1])
        b_wide = sb("b_wide", [P, P])
        bias_in = sb("bias_in", [P, 4])
        bias_col = sb("bias_col", [P, 4])
        hbg = sb("hbg", [P, 1])
        hbk = sb("hbk", [P, 1])
        bv_raw = sb("bv_raw", [P, D])
        bv = sb("bv", [P, D])
        rw_raw = sb("rw_raw", [E, D])
        rwT = sb("rwT", [P, E])
        rb = sb("rb", [P, E])
        temp = sb("temp", [P, 1])
        temp_c = sb("temp_c", [P, 1])
        rtemp = sb("rtemp", [P, 1])
        w_gp = sb("w_gp", [P, E, 2 * FF])
        w_o = sb("w_o", [P, E, FB, D])

        stats = sb("stats", [P, NT, 6])
        m_sum = sb("m_sum", [P, NT])
        m_dif = sb("m_dif", [P, NT])
        m_dif2 = sb("m_dif2", [P, NT])
        m_sq = sb("m_sq", [P, NT])
        va = sb("va", [P, 2, NT])
        ra = sb("ra", [P, NT])
        v2 = sb("v2", [P, NT])
        sq = sb("sq", [P, 2, NT])
        rs = sb("rs", [P, 2, NT])
        r12 = sb("r12", [P, NT])
        z = sb("z", [P, 2, G, D])
        zTg = sb("zTg", [P, 2, G, P])

        rA = sb("rA", [P, NT, E])
        rB = sb("rB", [P, NT, E])
        rC = sb("rC", [P, NT, E])
        rank = sb("rank", [P, E])
        t64 = sb("t64", [P, NT])
        u64 = sb("u64", [P, NT])
        v64 = sb("v64", [P, NT])
        cmax = sb("cmax", [NT, 1])
        diag = sb("diag", [NT, NT])

        expert_no = sb("expert_no", [P, E])
        class_no = sb("class_no", [P, K])
        pair_of = sb("pair_of", [P, 2, K])
        part_no = sb("part_no", [P, 1])
        ones_h = sb("ones_h", [P, P], BF16)
        before_h = sb("before_h", [P, P], BF16)
        wide = sb("wide", [P, 2 * K * NT])
        slot_w = wide[:, 0:K * NT].rearrange("p (k t) -> p k t", t=NT)
        member = wide[:, K * NT:3 * K * NT // 2].bitcast(BF16).rearrange("p (k t) -> p k t", t=NT)
        tile_before = wide[0:NT, 3 * K * NT // 2:2 * K * NT].bitcast(BF16).rearrange("p (k t) -> p k t", t=NT)
        tile_sum = sb("tile_sum", [NT, K], BF16)
        class_sum = sb("class_sum", [K, 1], I32)
        class_tiles = sb("class_tiles", [K, 1], I32)
        class_tilesf = sb("class_tilesf", [K, 1])
        bounds_r = sb("bounds_r", [K, 2, K])
        bounds = sb("bounds", [P, 2, K])
        bounds_w = sb("bounds_w", [P, K])
        slot = sb("slot", [P, NT])
        slot_u = sb("slot_u", [P, NT], U32)
        in_class = sb("in_class", [P, 2, K])
        is_class = sb("is_class", [P, K])
        pairs_w = sb("pairs_w", [P, 2, K])
        pairs = sb("pairs", [P, 2])
        pair_row = sb("pair_row", [1, P, 2], I32)
        zeros = sb("zeros", [P, ROW])

        xr = sb("xr", [P, G, D])
        th, sg, kg, ek, rk, eq, rq = (wide[:, a * GW:(a + 1) * GW] for a in range(7))
        kp = sb("kp", [P, 2, G, P])
        qp = sb("qp", [P, 2, G, P])
        v1 = sb("v1", [P, 2, G, D1])
        ktok = sb("ktok", [P, G, P])
        scores = sb("scores", [P, 2, G, P])
        state = sb("state", [P, C, D1])
        den = sb("den", [P, G])
        rden = sb("rden", [P, G])

        row = sb("row", [P, TILES, ROW])
        xT_high = sb("xT_high", [P, 2, P], F32R)
        xT_low = sb("xT_low", [P, 2, P], F32R)
        y = sb("y", [P, TILES, D])
        base = xr[:, 0:TILES, :]
        base_row = sb("base_row", [P, TILES], U32)
        y_row = sb("y_row", [P, TILES], U32)
        relu = sb("relu", [P, 2, FF])
        h = sb("h", [P, 2, FF])
        hT = sb("hT", [P, 2, FB, P])
        with nc.sbuf_tensor("rows", [P, NT, ROW], F32) as rows:
            pass
        w_high = sb("w_high", [P, E, 2 * FF], F32R)
        w_low = sb("w_low", [P, E, 2 * FF], F32R)

        psum = ctx.enter_context(nc.psum_tensor("psum", [P, 8, 512], F32))

        x_in = [sem("x_in0"), sem("x_in1")]
        w_loaded = sem("w_loaded")
        ew_loaded = sem("ew_loaded")
        const_ready = sem("const_ready")
        prep_pe = sem("prep_pe")
        prep_dve = sem("prep_dve")
        stat_step = sem("stat_step")
        sqrt_out = sem("sqrt_out")
        route_dve = sem("route_dve")
        route_act = sem("route_act")
        route_pe = sem("route_pe")
        cleared = sem("cleared")
        scattered = sem("scattered")
        row_in = [sem(f"row_in{q}") for q in range(TILES)]
        y_out = [sem(f"y_out{q}") for q in range(TILES)]
        base_in = [sem(f"base_in{q}") for q in range(TILES)]
        going = sem("going")
        w_split = sem("w_split")
        base_stored = sem("base_stored")

        def steps(names):
            return [sem(name) for name in names.split()]

        pool_steps = z_kept, xr_done, base_ready = steps("z_kept xr_done base_ready")
        act_steps = (zT_saved, zT_kept, th_done, ek_done, rq_done, kt_saved, s_saved, relu_done, hT_saved) = steps(
            "zT_saved zT_kept th_done ek_done rq_done kt_saved s_saved relu_done hT_saved")
        dve_steps = (z_ready, logit_saved, za_ready, sg_done, kg_done, kp_done, qp_done, v_saved, a_masked, o_used,
                     rden_step, h_done, xT_rounded, xT_ready, y_saved, base_row_ready) = steps(
            "z_ready logit_saved za_ready sg_done kg_done kp_done qp_done v_saved a_masked o_used "
            "rden_step h_done xT_rounded xT_ready y_saved base_row_ready")
        pe_steps = (zT_ready, logit_ready, g_ready, k_ready, q_ready, v_ready, a_ready, kt_ready, s_ready, o_ready,
                    row_turned, gu_ready, hT_ready, wo_done) = steps(
            "zT_ready logit_ready g_ready k_ready q_ready v_ready a_ready kt_ready s_ready o_ready "
            "row_turned gu_ready hT_ready wo_done")

        def start(eng, mine):
            for s in mine:
                eng.sem_inc(s, AHEAD)

        def wait(eng, s, count):
            if not isinstance(count, int) or count > 0:
                eng.wait_ge(s, count + AHEAD)

        def loop_and_last(eng, n, body):
            with eng.Fori(0, n - 1) as i:
                body(i, False)
            body(n - 1, True)

        WQ, WK, WV, WG = (slice(i * D, (i + 1) * D) for i in range(4))
        PAIRS = B // 2
        NCONST = 7 + 5 + 2 * (E - 1) + 3
        ROUND = 11
        ROW_SHIFTED, ROW_SUMMED, TOKEN_MAX, DIAG, COL_SHIFTED, COL_SUMMED = 2, 3, 5, 7, 9, 10

        def route_step(s, place=0):
            return 2 + ROUND * s + place

        MEMBER_STEP = route_step(SINKHORN_ITERS) + 4 + 11 + 1 + 6 + 14
        TILE_SUM_STEP = MEMBER_STEP + 1
        TILE_BEFORE_STEP = TILE_SUM_STEP + 1
        BOUNDS_STEP = TILE_BEFORE_STEP + 4
        SLOTS_STEP = BOUNDS_STEP + 6
        PAIRS_STEP = SLOTS_STEP + 4
        PAIR_ROW_STEP = PAIRS_STEP + 1
        ROUTE_PE_TILES = 3 * SINKHORN_ITERS + 1
        ROUTE_PE_CLASSES = ROUTE_PE_TILES + 1
        ROUTE_PE_BOUNDS = ROUTE_PE_CLASSES + 2
        ROUTE_PE_PAIRS = ROUTE_PE_BOUNDS + 1

        block = ctx.enter_context(nc.Block())

        @block.sync
        def _(sp):
            def load_x(b, j):
                sp.dma_start(xs[:, bass.ds(b * C, C), :], x_view[bass.ds(b, 1)]
                             .rearrange("a p c d -> p (a c) d")).then_inc(x_in[j], 16)

            load_x(0, 0)
            load_x(1, 1)
            with sp.Fori(1, PAIRS) as i:
                for j in range(2):
                    sp.wait_ge(x_in[j], 16 * i)
                    load_x(2 * i + j, j)
            sp.dma_start(w_gp[:, :, 0:FF], wg.rearrange("e d f -> d e f")).then_inc(ew_loaded, 16)
            sp.dma_start(w_gp[:, :, FF:2 * FF], wp.rearrange("e d f -> d e f")).then_inc(ew_loaded, 16)
            sp.dma_start(w_o[:, :, :, :], wo.rearrange("e (b p) d -> p e b d", p=P)).then_inc(ew_loaded, 16)
            sp.wait_ge(const_ready, NCONST)
            sp.dma_start(sorted_rows.rearrange("(n p) r -> p n r", p=P),
                         zeros[:].unsqueeze(1).to_broadcast([P, NS, ROW])).then_inc(cleared, 16)

            def load_row(m, q):
                i = m * TILES + q
                wait(sp, h_done, 2 * (i - TILES + 1))
                sp.dma_start(row[:, q, :], sorted_rows.rearrange("(n p) r -> n p r", p=P)[bass.ds(i, 1)]
                             .rearrange("a p r -> p (a r)")).then_inc(row_in[q], 16)
            sp.wait_ge(scattered, 16 * NT)
            for q in range(TILES):
                load_row(0, q)
            for b in range(B):
                wait(sp, o_used, GB * (b + 1))
                sp.dma_start(base_rows[b * T:(b + 1) * T, :].rearrange("(c p) d -> p c d", p=P),
                             xs[:, b * C:(b + 1) * C, :]).then_inc(base_stored, 16)
            with sp.Fori(1, NS // TILES) as m:
                for q in range(TILES):
                    load_row(m, q)

        @block.gpsimd
        def _(pool):
            start(pool, pool_steps)
            pool.memset(ones[:], 1.0).then_inc(const_ready, 1)
            pool.memset(ones_h[:], 1.0).then_inc(const_ready, 1)
            pool.memset(ident[:], 0.0).then_inc(const_ready, 1)
            pool.memset(causal[:], 1.0).then_inc(const_ready, 1)
            pool.memset(before_h[:], 1.0).then_inc(const_ready, 1)
            pool.memset(v1[:], 1.0).then_inc(const_ready, 1)
            pool.memset(zeros[:], 0.0).then_inc(const_ready, 1)

            def count_up(out, pattern, base, per_partition=0):
                pool.iota(out, pattern=pattern, base=base, channel_multiplier=per_partition,
                          allow_small_or_imprecise_dtypes=True).then_inc(const_ready, 1)

            count_up(rank[:], [[-1, E]], E)
            count_up(expert_no[:], [[1, E]], 0)
            count_up(class_no[:], [[1, K]], 0)
            count_up(part_no[:], [[1, 1]], 0, 1)
            count_up(rows[:, :, D + 2], [[-P, NT]], NTOK, -1)
            first = 0
            for e in range(E - 1):
                count_up(pair_of[:, 0, first:first + E - 1 - e], [[0, E - 1 - e]], e)
                count_up(pair_of[:, 1, first:first + E - 1 - e], [[1, E - 1 - e]], e + 1)
                first += E - 1 - e
            pool.wait_ge(const_ready, NCONST - 3)
            pool.affine_select(out=ident[:], in_=ident[:], compare_op=ALU.not_equal, fill=1.0, base=0,
                               pattern=[[-1, P]], channel_multiplier=1).then_inc(const_ready, 1)
            pool.affine_select(out=causal[:], in_=causal[:], compare_op=ALU.is_ge, fill=0.0, base=0,
                               pattern=[[1, P]], channel_multiplier=-1).then_inc(const_ready, 1)
            pool.affine_select(out=before_h[:], in_=before_h[:], compare_op=ALU.is_ge, fill=0.0, base=-1,
                               pattern=[[1, P]], channel_multiplier=-1).then_inc(const_ready, 1)

            with pool.Fori(0, PAIRS) as i:
                for gl in range(2 * GB):
                    n = 2 * GB * i + gl
                    wait(pool, z_ready, n + 1)
                    pool.tensor_copy(rows[:, bass.ds(n * G, G), 0:D], z[:, gl % 2]).then_inc(z_kept, 1)

            pool.wait_ge(prep_dve, 8)
            with pool.Fori(0, NG) as n:
                tiles = bass.ds(n * G, G)
                wait(pool, base_ready, n)
                pool.tensor_tensor(xr[:], xs[:, tiles, :], r1p[:, tiles].unsqueeze(2).to_broadcast([P, G, D]),
                                   ALU.mult).then_inc(xr_done, 1)
                wait(pool, xr_done, n + 1)
                pool.tensor_tensor(xs[:, tiles, :], xr[:], mr[:, tiles].unsqueeze(2).to_broadcast([P, G, D]),
                                   ALU.subtract).then_inc(base_ready, 1)

            pool.wait_ge(cleared, 16)
            wait(pool, z_kept, NG)
            pool.wait_ge(route_dve, SLOTS_STEP)
            for i in range(NT):
                pool.indirect_dma_start(sorted_rows, bass.IndirectOffsetOnAxis(ap=slot_u[:, i:i + 1], axis=0),
                                        rows[:, i, :], None).then_inc(scattered, 16)

            pool.wait_ge(scattered, 16 * NT)
            pool.wait_ge(ew_loaded, 48)
            pool.tensor_copy(w_high[:], w_gp[:]).then_inc(w_split, 1)
            pool.wait_ge(w_split, 1)
            pool.tensor_tensor(w_low[:], w_gp[:], w_high[:].bitcast(F32), ALU.subtract).then_inc(w_split, 1)

            def fetch_base(i, q):
                wait(pool, base_row_ready, i + 1)
                pool.sem_inc(going, 1)
                pool.indirect_dma_start(base[:, q, :], None, base_rows,
                                        bass.IndirectOffsetOnAxis(ap=base_row[:, q:q + 1], axis=0),
                                        bounds_check=NTOK - 1, oob_is_err=False).then_inc(base_in[q], 16)

            def put_out(i, q):
                wait(pool, y_saved, i + 1)
                pool.sem_inc(going, 1)
                pool.indirect_dma_start(out_rows, bass.IndirectOffsetOnAxis(ap=y_row[:, q:q + 1], axis=0),
                                        y[:, q, :], None, bounds_check=NTOK - 1, oob_is_err=False)\
                    .then_inc(y_out[q], 16)

            def four_tiles(m, is_last):
                for q in range(TILES):
                    i = m * TILES + q
                    put_out(i, q)
                    if not (is_last and q > 0):
                        fetch_base(i + TILES - 1, (q - 1) % TILES)

            pool.wait_ge(base_stored, 16 * B)
            wait(pool, base_ready, NG)
            for q in range(TILES - 1):
                fetch_base(q, q)
            loop_and_last(pool, NS // TILES, four_tiles)
            for q in range(TILES):
                pool.wait_ge(y_out[q], 16 * (NS // TILES))

        @block.scalar
        def _(act):
            start(act, act_steps)
            act.dma_start(w_raw[:, 0:3 * D], qkv_w).then_inc(w_loaded, 16)
            act.dma_start(w_raw[:, WG], gate_w).then_inc(w_loaded, 16)
            act.dma_start(g_col[:], ln_g.rearrange("(p a) -> p a", a=1)).then_inc(w_loaded, 16)
            act.dma_start(b_col[:], ln_b.rearrange("(p a) -> p a", a=1)).then_inc(w_loaded, 16)
            act.dma_start(bias_in[:, 0:3], qkv_b.rearrange("(a p) -> p a", p=P), allow_slow_non_contiguous=True).then_inc(w_loaded, 16)
            act.dma_start(bias_in[:, 3:4], gate_b.rearrange("(p a) -> p a", a=1)).then_inc(w_loaded, 16)
            act.dma_start(bv_raw[:], qkv_b[2 * D:3 * D].partition_broadcast(P)).then_inc(w_loaded, 16)
            act.dma_start(rw_raw[:], router_w).then_inc(w_loaded, 16)
            act.dma_start(rb[:], router_b.partition_broadcast(P)).then_inc(w_loaded, 16)
            act.dma_start(temp[:], temperature.partition_broadcast(P)).then_inc(w_loaded, 16)

            act.wait_ge(stat_step, 6)
            act.activation(sq[:], va[:], ACT.Sqrt).then_inc(sqrt_out, 1)
            with act.Fori(0, PAIRS) as i:
                for gl in range(2 * GB):
                    n = 2 * GB * i + gl
                    wait(act, zT_ready, n + 1)
                    wait(act, logit_ready, n - 1)
                    group_zT = psum[:, gl % 2, :].rearrange("p (g t) -> p g t", g=G)
                    act.activation(zTg[:, gl % 2], group_zT, ACT.Copy).then_inc(zT_saved, 1)
                    act.activation(zT[:, bass.ds(n * G, G), :], group_zT, ACT.Copy).then_inc(zT_kept, 1)

            for s in range(SINKHORN_ITERS):
                act.wait_ge(route_dve, route_step(s, ROW_SHIFTED))
                act.activation(rB[:], rA[:], ACT.Exp).then_inc(route_act, 1)
                act.wait_ge(route_dve, route_step(s, ROW_SUMMED))
                act.activation(u64[:], t64[:], ACT.Ln).then_inc(route_act, 1)
                act.wait_ge(route_dve, route_step(s, COL_SHIFTED))
                act.activation(rB[:], rA[:], ACT.Exp).then_inc(route_act, 1)
                act.wait_ge(route_pe, 3 * s + 3)
                act.activation(u64[:], psum[:, 2, 0:NT], ACT.Ln).then_inc(route_act, 1)
            act.wait_ge(route_dve, route_step(SINKHORN_ITERS))
            act.activation(rB[:], rC[:], ACT.Exp).then_inc(route_act, 1)

            def tanh_gate(n):
                wait(act, g_ready, n + 1)
                wait(act, sg_done, n)
                act.activation(th, psum[:, 0, :], ACT.Tanh, bias=hbg[:], scale=0.5).then_inc(th_done, 1)

            def exp_query(n):
                wait(act, q_ready, n + 1)
                wait(act, qp_done, n)
                act.activation(eq, psum[:, 2, :], ACT.Exp, bias=bias_col[:, 0:1])
                act.activation(rq, psum[:, 2, :], ACT.Relu, bias=bias_col[:, 0:1]).then_inc(rq_done, 1)

            def exp_key(n):
                wait(act, kg_done, n + 1)
                wait(act, kp_done, n)
                act.activation(ek, kg, ACT.Exp)
                act.activation(rk, kg, ACT.Relu).then_inc(ek_done, 1)

            def copy_state(b, hb, c):
                cb = G * hb + c
                if cb == C - 1:
                    return
                wait(act, s_ready, (C - 1) * b + cb + 1)
                wait(act, o_ready, GB * b + hb - 1 + (1 if cb + 1 == G else 0))
                act.activation(state[:, cb + 1, :], psum[:, 5, 0:D1], ACT.Copy).then_inc(s_saved, 1)

            def batch(b, is_last):
                for hb in range(GB):
                    n = GB * b + hb
                    ahead = not (is_last and hb == GB - 1)
                    wait(act, kt_ready, n + 1)
                    wait(act, s_ready, (C - 1) * b + G * hb)
                    act.activation(ktok[:], psum[:, 3, :].rearrange("p (g t) -> p g t", g=G), ACT.Copy)\
                       .then_inc(kt_saved, 1)
                    copy_state(b, hb, 0)
                    if ahead:
                        tanh_gate(n + 1)
                    copy_state(b, hb, 1)
                    copy_state(b, hb, 2)
                    if ahead:
                        exp_query(n + 1)
                        exp_key(n + 1)
                    copy_state(b, hb, 3)

            act.wait_ge(prep_dve, 8)
            tanh_gate(0)
            exp_query(0)
            exp_key(0)
            loop_and_last(act, B, batch)

            def save_hT(k, kb):
                wait(act, hT_ready, k + 1)
                act.activation(hT[:, kb], psum[:, 2 + kb, 0:FF].rearrange("p (b t) -> p b t", b=FB),
                               ACT.Copy).then_inc(hT_saved, 1)

            def save_relu(i, q, e):
                wait(act, gu_ready, 2 * i + e + 1)
                act.activation(relu[:, e, :], psum[:, e, 0:FF], ACT.Relu,
                               scale=row[:, q, D + e:D + e + 1]).then_inc(relu_done, 1)

            def four_tiles(m, is_last):
                for q in range(TILES):
                    i = m * TILES + q
                    save_relu(i, q, 1)
                    save_hT(2 * i, 0)
                    if not (is_last and q == TILES - 1):
                        save_relu(i + 1, (q + 1) % TILES, 0)
                    save_hT(2 * i + 1, 1)

            save_relu(0, 0, 0)
            loop_and_last(act, NS // TILES, four_tiles)

        @block.vector
        def _(dve):
            start(dve, dve_steps)
            dve.wait_ge(w_loaded, 16 * 10)
            dve.wait_ge(const_ready, NCONST)
            dve.tensor_scalar(w_in[:, WQ], w_raw[:, WQ], g_col[:], None, ALU.mult)
            dve.tensor_scalar(w_in[:, 2 * D:4 * D], w_raw[:, 2 * D:4 * D], g_col[:], None, ALU.mult)\
               .then_inc(prep_dve, 1)
            dve.tensor_scalar(b_wide[:], ones[:], b_col[:], None, ALU.mult)
            dve.tensor_scalar(w_in[:, WK], w_raw[:, WK], g_col[:], 0.5, ALU.mult, ALU.mult).then_inc(prep_dve, 1)
            dve.wait_ge(prep_pe, 1)
            dve.tensor_tensor(bias_col[:], psum[:, 0, 0:4], bias_in[:], ALU.add).then_inc(prep_dve, 1)
            dve.tensor_tensor(bv[:], psum[:, 1, 0:D], bv_raw[:], ALU.add)
            dve.tensor_copy(rwT[:], psum[:, 2, 0:E])
            dve.tensor_scalar(temp_c[:], temp[:], TEMP_MIN, None, ALU.max).then_inc(prep_dve, 1)
            dve.wait_ge(prep_dve, 4)
            dve.tensor_scalar(hbg[:], bias_col[:, 3:4], 0.5, None, ALU.mult)
            dve.tensor_scalar(hbk[:], bias_col[:, 1:2], 0.5, None, ALU.mult)
            dve.reciprocal(rtemp[:], temp_c[:]).then_inc(prep_dve, 1)

            for ti in range(NT):
                if ti % C == 0:
                    dve.wait_ge(x_in[ti // C % 2], 16 * (ti // C // 2 + 1))
                dve.bn_stats(stats[:, ti, :], xs[:, ti, :])
            stat = [0]

            def stat_link(*these):
                stat[0] += 1
                these[-1].then_inc(stat_step, 1)
                dve.wait_ge(stat_step, stat[0])

            stat_link(dve.engine_nop())
            stat_link(dve.tensor_tensor(m_sum[:], stats[:, :, 1], stats[:, :, 4], ALU.add),
                      dve.tensor_tensor(m_dif[:], stats[:, :, 1], stats[:, :, 4], ALU.subtract),
                      dve.tensor_tensor(m_sq[:], stats[:, :, 2], stats[:, :, 5], ALU.add))
            stat_link(dve.scalar_tensor_tensor(m_dif2[:], m_dif[:], 0.25, m_dif[:], ALU.mult, ALU.mult),
                      dve.tensor_scalar(mean[:], m_sum[:], 0.5, None, ALU.mult))
            stat_link(dve.scalar_tensor_tensor(var[:], m_sq[:], 1.0 / D, m_dif2[:], ALU.mult, ALU.add))
            stat_link(dve.tensor_scalar(va[:, 0, :], var[:], LN_EPS, None, ALU.add))
            dve.reciprocal(ra[:], va[:, 0, :]).then_inc(prep_dve, 1)
            dve.wait_ge(prep_dve, 6)
            dve.tensor_tensor(v2[:], var[:], ra[:], ALU.mult).then_inc(prep_dve, 1)
            dve.wait_ge(prep_dve, 7)
            stat_link(dve.tensor_scalar(va[:, 1, :], v2[:], LN_EPS, None, ALU.add))
            dve.wait_ge(sqrt_out, 1)
            stat_link(dve.reciprocal(rs[:], sq[:]))
            stat_link(dve.tensor_tensor(r12[:], rs[:, 0, :], rs[:, 1, :], ALU.mult))
            dve.tensor_tensor(mr[:], mean[:], rs[:, 0, :], ALU.mult)
            dve.tensor_scalar(r1p[:], rs[:, 0, :], 1.0, None, ALU.add).then_inc(prep_dve, 1)

            def save_logits(b, j):
                wait(dve, logit_ready, GB * (b + 1))
                tiles = bass.ds(b * C, C)
                dve.tensor_tensor(gate[:, tiles, :], psum[:, 2 + j, 0:C * E].rearrange("p (c e) -> p c e", e=E),
                                  sq[:, 1, tiles].unsqueeze(2).to_broadcast([P, C, E]), ALU.mult)\
                   .then_inc(logit_saved, 1)

            def normalise(n, hb):
                wait(dve, zT_ready, n - 1)
                wait(dve, z_kept, n - 1)
                for t in range(G):
                    ti = n * G + t
                    last = dve.tensor_scalar(z[:, hb, t, :], xs[:, bass.ds(ti, 1), :].rearrange("p a d -> p (a d)"),
                                             mean[:, bass.ds(ti, 1)], r12[:, bass.ds(ti, 1)],
                                             ALU.subtract, ALU.mult)
                last.then_inc(z_ready, 1)

            def pair_of_batches(i, first):
                for j in range(2):
                    normalise(2 * GB * i + GB * j, 0)
                    normalise(2 * GB * i + GB * j + 1, 1)
                    if not (first and j == 0):
                        save_logits(2 * i + j - 1, 1 - j)
            pair_of_batches(0, True)
            with dve.Fori(1, PAIRS) as i:
                pair_of_batches(i, False)
            save_logits(B - 1, 1)

            chain = [0]

            def link(ins):
                chain[0] += 1
                ins.then_inc(route_dve, 1)
                dve.wait_ge(route_dve, chain[0])

            def over_e(a):
                return a.unsqueeze(2).to_broadcast([P, NT, E])

            def by_batch(a):
                return a.rearrange("p (b c) e -> p b c e", c=C)

            def over_c(a):
                return a.rearrange("p (b e) -> p b e", e=E).unsqueeze(2).to_broadcast([P, B, C, E])

            wait(dve, logit_saved, B)
            link(dve.tensor_tensor(rA[:], gate[:], rb[:].unsqueeze(1).to_broadcast([P, NT, E]), ALU.add))
            link(dve.tensor_scalar(rC[:], rA[:], rtemp[:], None, ALU.mult))
            acts = 0
            for s in range(SINKHORN_ITERS):
                link(dve.tensor_reduce(t64[:], rC[:], AX_X, ALU.max))
                link(dve.tensor_tensor(rA[:], rC[:], over_e(t64[:]), ALU.subtract))
                acts += 1
                dve.wait_ge(route_act, acts)
                link(dve.tensor_reduce(t64[:], rB[:], AX_X, ALU.add))
                acts += 1
                dve.wait_ge(route_act, acts)
                link(dve.tensor_tensor(rC[:], rA[:], over_e(u64[:]), ALU.subtract))
                link(dve.tensor_reduce(t64[:].rearrange("p (b e) -> p b e", e=E),
                                       by_batch(rC[:]).rearrange("p b c e -> p b e c"), AX_X, ALU.max))
                dve.wait_ge(route_pe, 3 * s + 1)
                link(dve.tensor_reduce(cmax[:], psum[0:NT, 0, 0:P], AX_X, ALU.max))
                link(dve.tensor_scalar(diag[:], ident[0:NT, 0:NT], cmax[:], None, ALU.mult))
                dve.wait_ge(route_pe, 3 * s + 2)
                link(dve.tensor_copy(v64[:], psum[:, 1, 0:NT]))
                link(dve.tensor_tensor(by_batch(rA[:]), by_batch(rC[:]), over_c(v64[:]), ALU.subtract))
                acts += 1
                dve.wait_ge(route_act, acts)
                link(dve.tensor_reduce(t64[:].rearrange("p (b e) -> p b e", e=E),
                                       by_batch(rB[:]).rearrange("p b c e -> p b e c"), AX_X, ALU.add))
                acts += 1
                dve.wait_ge(route_act, acts)
                link(dve.tensor_tensor(by_batch(rC[:]), by_batch(rA[:]), over_c(u64[:]), ALU.subtract))
                assert chain[0] == route_step(s + 1)
            acts += 1
            dve.wait_ge(route_act, acts)
            link(dve.tensor_reduce(t64[:], rB[:], AX_X, ALU.add))
            link(dve.tensor_scalar(u64[:], t64[:], GATE_EPS, None, ALU.add))
            link(dve.reciprocal(v64[:], u64[:]))
            link(dve.tensor_tensor(gate[:], rB[:], over_e(v64[:]), ALU.mult))
            ranks = rank[:].unsqueeze(1).to_broadcast([P, NT, E])

            def top(src, vmax, onehot):
                link(dve.tensor_reduce(vmax, src, AX_X, ALU.max))
                link(dve.tensor_tensor(rB[:], src, over_e(vmax), ALU.is_ge))
                link(dve.tensor_tensor(rB[:], rB[:], ranks, ALU.mult))
                link(dve.tensor_reduce(v64[:], rB[:], AX_X, ALU.max))
                link(dve.tensor_tensor(onehot, rB[:], over_e(v64[:]), ALU.is_equal))

            top(gate[:], t64[:], rA[:])
            link(dve.scalar_tensor_tensor(rC[:].rearrange("p t e -> p (t e)"), rA[:].rearrange("p t e -> p (t e)"),
                                          -BIG, gate[:].rearrange("p t e -> p (t e)"), ALU.mult, ALU.add))
            top(rC[:], u64[:], rC[:])
            link(dve.tensor_tensor(rA[:], rA[:], rC[:], ALU.add))
            link(dve.tensor_tensor(t64[:], t64[:], u64[:], ALU.add))
            link(dve.tensor_scalar(t64[:], t64[:], GATE_EPS, None, ALU.add))
            link(dve.reciprocal(u64[:], t64[:]))
            link(dve.tensor_tensor(u64[:], u64[:], sq[:, 1, :], ALU.mult))
            link(dve.tensor_tensor(u64[:], u64[:], sq[:, 1, :], ALU.mult))
            link(dve.tensor_tensor(gate[:], gate[:], over_e(u64[:]), ALU.mult))

            numbers = expert_no[:].unsqueeze(1).to_broadcast([P, NT, E])
            link(dve.tensor_tensor(rB[:], rA[:], ranks, ALU.mult))
            link(dve.tensor_reduce(t64[:], rB[:], AX_X, ALU.max))
            link(dve.tensor_tensor(rC[:], rB[:], over_e(t64[:]), ALU.is_equal))
            link(dve.tensor_tensor(rB[:], rC[:], gate[:], ALU.mult))
            link(dve.tensor_reduce(rows[:, :, D], rB[:], AX_X, ALU.add))
            link(dve.tensor_tensor(rB[:], rA[:], numbers, ALU.mult))
            link(dve.tensor_reduce(u64[:], rB[:], AX_X, ALU.max))
            link(dve.tensor_tensor(rC[:], rB[:], over_e(u64[:]), ALU.is_equal))
            link(dve.tensor_tensor(rB[:], rC[:], gate[:], ALU.mult))
            link(dve.tensor_reduce(rows[:, :, D + 1], rB[:], AX_X, ALU.add))
            link(dve.tensor_scalar(v64[:], t64[:], -0.5, 1.5, ALU.mult, ALU.add))
            link(dve.tensor_tensor(v64[:], v64[:], t64[:], ALU.mult))
            link(dve.scalar_tensor_tensor(v64[:], v64[:], float(K - E - 1), u64[:], ALU.add, ALU.add))
            link(dve.tensor_tensor(member, v64[:].unsqueeze(1).to_broadcast([P, K, NT]),
                                   class_no[:].unsqueeze(2).to_broadcast([P, K, NT]), ALU.is_equal))
            assert chain[0] == MEMBER_STEP
            dve.wait_ge(route_pe, ROUTE_PE_TILES)
            link(dve.tensor_copy(tile_sum[:], psum[0:NT, 0, 0:K]))
            assert chain[0] == TILE_SUM_STEP
            link(dve.tensor_tensor(tile_before, tile_sum[:].unsqueeze(2).to_broadcast([NT, K, NT]),
                                   before_h[0:NT, 0:NT].unsqueeze(1).to_broadcast([NT, K, NT]), ALU.mult))
            assert chain[0] == TILE_BEFORE_STEP
            dve.wait_ge(route_pe, ROUTE_PE_CLASSES)
            link(dve.tensor_scalar(class_sum[:], psum[0:K, 1, 0:1], float(P - 1), None, ALU.add))
            link(dve.tensor_scalar(class_tiles[:], class_sum[:], P.bit_length() - 1, None, ALU.arith_shift_right))
            link(dve.tensor_copy(class_tilesf[:], class_tiles[:]))
            dve.tensor_scalar(bounds_r[:, 1, :], causal[0:K, 0:K], class_tilesf[:], None, ALU.mult)
            link(dve.tensor_scalar(bounds_r[:, 0, :], before_h[0:K, 0:K], class_tilesf[:], None, ALU.mult))
            assert chain[0] == BOUNDS_STEP
            dve.wait_ge(route_pe, ROUTE_PE_BOUNDS)
            link(dve.tensor_copy(bounds[:].rearrange("p a k -> p (a k)"), psum[:, 2, 0:2 * K]))
            link(dve.tensor_scalar(bounds_w[:], bounds[:, 0, :], float(P), None, ALU.mult))
            for g in range(K // KB):
                classes = slice(g * KB, (g + 1) * KB)
                last = dve.tensor_tensor(slot_w[:, classes, :],
                                         psum[:, 4 + g, 0:KB * NT].rearrange("p (k t) -> p k t", t=NT),
                                         bounds_w[:, classes].unsqueeze(2).to_broadcast([P, KB, NT]), ALU.add)
            link(last)
            link(dve.tensor_tensor(slot_w, slot_w, member, ALU.mult))
            link(dve.tensor_reduce(slot[:], slot_w.rearrange("p k t -> p t k"), AX_X, ALU.add))
            link(dve.tensor_copy(slot_u[:], slot[:]))
            assert chain[0] == SLOTS_STEP
            link(dve.tensor_scalar(in_class[:], bounds[:], part_no[:], None, ALU.is_le))
            link(dve.tensor_tensor(is_class[:], in_class[:, 0, :], in_class[:, 1, :], ALU.subtract))
            link(dve.tensor_tensor(pairs_w[:], pair_of[:], is_class[:].unsqueeze(1).to_broadcast([P, 2, K]),
                                   ALU.mult))
            link(dve.tensor_reduce(pairs[:], pairs_w[:], AX_X, ALU.add))
            assert chain[0] == PAIRS_STEP
            dve.wait_ge(route_pe, ROUTE_PE_PAIRS)
            link(dve.tensor_copy(pair_row[:].rearrange("o t a -> o a t"),
                                 psum[0:1, 3, 0:2 * P].rearrange("o (a t) -> o a t", a=2)))
            assert chain[0] == PAIR_ROW_STEP

            def finish(n):
                wait(dve, o_ready, n + 1)
                for j in range(2):
                    o2 = psum[:, 6 + j, 0:2 * D1].rearrange("p (k x) -> p k x", x=D1)
                    last = dve.tensor_scalar(den[:, 2 * j:2 * j + 2].unsqueeze(2), o2[:, :, D:D1], DEN_EPS, None,
                                             ALU.add)
                last.then_inc(rden_step, 1)
                wait(dve, rden_step, 2 * n + 1)
                dve.reciprocal(rden[:], den[:]).then_inc(rden_step, 1)
                wait(dve, rden_step, 2 * n + 2)
                wait(dve, base_ready, n + 1)
                for t in range(G):
                    o = psum[:, 6 + t // 2, (t % 2) * D1:(t % 2) * D1 + D]
                    acc = xs[:, bass.ds(n * G + t, 1), :].rearrange("p a d -> p (a d)")
                    last = dve.scalar_tensor_tensor(acc, o, rden[:, t:t + 1], acc, ALU.mult, ALU.add)
                last.then_inc(o_used, 1)

            def fetch_zT(n, hb):
                wait(dve, v_ready, n - 1)
                dve.tensor_copy(zTg[:, hb], zT[:, bass.ds(n * G, G), :]).then_inc(za_ready, 1)

            def group(n, hb, is_last=False):
                wait(dve, th_done, n + 1)
                dve.tensor_scalar(sg, th, 1.0, None, ALU.add).then_inc(sg_done, 1)
                wait(dve, k_ready, n + 1)
                wait(dve, sg_done, n + 1)
                wait(dve, ek_done, n)
                dve.scalar_tensor_tensor(kg, psum[:, 1, :], hbk[:], sg, ALU.add, ALU.mult)\
                   .then_inc(kg_done, 1)
                wait(dve, rq_done, n + 1)
                if not is_last:
                    fetch_zT(n + 1, 1 - hb)
                wait(dve, o_ready, n - 1)
                dve.scalar_tensor_tensor(qp[:, hb].rearrange("p g t -> p (g t)"), eq, 1.0, rq,
                                         ALU.min, ALU.add).then_inc(qp_done, 1)
                wait(dve, ek_done, n + 1)
                dve.scalar_tensor_tensor(kp[:, hb].rearrange("p g t -> p (g t)"), ek, 1.0, rk,
                                         ALU.min, ALU.add).then_inc(kp_done, 1)
                wait(dve, v_ready, n + 1)
                dve.tensor_tensor(v1[:, hb, :, 0:D], psum[:, 3, :].rearrange("p (g d) -> p g d", g=G),
                                  bv[:].unsqueeze(1).to_broadcast([P, G, D]), ALU.add).then_inc(v_saved, 1)

            def mask(n, hb):
                wait(dve, a_ready, n + 1)
                dve.tensor_tensor(scores[:, hb], psum[:, 4, :].rearrange("p (g t) -> p g t", g=G),
                                  causal[:].unsqueeze(1).to_broadcast([P, G, P]), ALU.mult).then_inc(a_masked, 1)

            wait(dve, zT_kept, NG)
            wait(dve, logit_ready, NG)
            fetch_zT(0, 0)
            group(0, 0)
            mask(0, 0)
            group(1, 1)
            finish(0)
            mask(1, 1)

            def batch(b, is_last):
                for hb in range(GB):
                    n = GB * b + hb
                    group(n, hb, is_last and hb == GB - 1)
                    finish(n - 1)
                    mask(n, hb)
            with dve.Fori(1, B - 1) as b:
                batch(b, False)
            batch(B - 1, True)
            finish(NG - 1)

            def save_xT(i, j):
                wait(dve, row_turned, i + 1)
                dve.tensor_copy(xT_high[:, j, :], psum[:, 6, 0:P]).then_inc(xT_rounded, 1)
                wait(dve, xT_rounded, i + 1)
                dve.tensor_tensor(xT_low[:, j, :], psum[:, 6, 0:P], xT_high[:, j, :].bitcast(F32), ALU.subtract)\
                   .then_inc(xT_ready, 1)

            def product(k, e):
                wait(dve, relu_done, k + 1)
                dve.tensor_tensor(h[:, e, :], relu[:, e, :], psum[:, e, FF:2 * FF], ALU.mult).then_inc(h_done, 1)

            def fetch_numbers(m, q):
                dve.wait_ge(row_in[q], 16 * (m + 1))
                dve.tensor_scalar(base_row[:, q:q + 1], row[:, q, D + 2:D + 3], -1.0, float(NTOK),
                                  ALU.mult, ALU.add).then_inc(base_row_ready, 1)

            def out_numbers(m, q):
                if not (isinstance(m, int) and m == 0):
                    dve.wait_ge(y_out[q], 16 * m)
                dve.tensor_scalar(y_row[:, q:q + 1], row[:, q, D + 2:D + 3], -1.0, float(NTOK), ALU.mult, ALU.add)

            def save_y(m, q, lag):
                q0, m0 = (q - lag) % TILES, m + (q - lag) // TILES
                wait(dve, wo_done, 2 * (m0 * TILES + q0 + 1))
                dve.wait_ge(base_in[q0], 16 * (m0 + 1))
                dve.tensor_tensor(y[:, q0, :], psum[:, 4 + q0 % 2, 0:D], base[:, q0, :], ALU.add)\
                   .then_inc(y_saved, 1)

            def four_tiles(m, is_first, is_last):
                for q in range(TILES):
                    i = m * TILES + q
                    out_numbers(m, q)
                    product(2 * i + 1, 1)
                    if not (is_first and q == 0):
                        save_y(m, q, 1)
                    if not (is_last and q == TILES - 1):
                        product(2 * i + 2, 0)
                    if not (is_last and q >= TILES - 2):
                        save_xT(i + 2, q % 2)
                        fetch_numbers(m + (q + 2) // TILES, (q + 2) % TILES)
            wait(dve, o_used, NG)
            save_xT(0, 0)
            save_xT(1, 1)
            fetch_numbers(0, 0)
            fetch_numbers(0, 1)
            product(0, 0)
            four_tiles(0, True, False)
            with dve.Fori(1, NS // TILES - 1) as m:
                four_tiles(m, False, False)
            four_tiles(NS // TILES - 1, False, True)
            save_y(NS // TILES - 1, TILES - 1, 0)

        @block.tensor
        def _(pe):
            start(pe, pe_steps)
            pe.wait_ge(w_loaded, 16 * 10)
            pe.wait_ge(const_ready, NCONST)
            pe.wait_ge(prep_dve, 2)
            for f in range(4):
                pe.matmul(psum[:, 0, f:f + 1], w_raw[:, f * D:(f + 1) * D], b_col[:], start=True, stop=True)
            pe.matmul(psum[:, 1, 0:D], b_wide[:], w_raw[:, WV], start=True, stop=True)
            pe.transpose(psum[:, 2, 0:E], rw_raw[:], ident[0:E, 0:E]).then_inc(prep_pe, 1)
            pe.wait_ge(prep_dve, 4)

            def turn_z(n, hb):
                wait(pe, z_ready, n + 1)
                wait(pe, zT_kept, n - 1)
                for t in range(G):
                    last = pe.transpose(psum[:, hb, t * P:(t + 1) * P], z[:, hb, t, :], ident[:])
                last.then_inc(zT_ready, 1)

            def score(b, j, hb):
                n = GB * b + hb
                wait(pe, zT_saved, n + 1)
                if hb == 0:
                    wait(pe, logit_saved, b - 1)
                for t in range(G):
                    c = G * hb + t
                    last = pe.matmul(psum[:, 2 + j, c * E:(c + 1) * E], zTg[:, hb, t, :], rwT[:],
                                     start=True, stop=True)
                last.then_inc(logit_ready, 1)

            def pair_of_batches(i, is_last):
                for j in range(2):
                    for hb in range(GB):
                        n = GB * (2 * i + j) + hb
                        if not (is_last and j == 1 and hb == GB - 1):
                            turn_z(n + 1, 1 - hb)
                        score(2 * i + j, j, hb)
            turn_z(0, 0)
            loop_and_last(pe, PAIRS, pair_of_batches)

            for s in range(SINKHORN_ITERS):
                pe.wait_ge(route_dve, route_step(s, TOKEN_MAX))
                pe.transpose(psum[0:NT, 0, 0:P], t64[:], ident[:]).then_inc(route_pe, 1)
                pe.wait_ge(route_dve, route_step(s, DIAG))
                pe.matmul(psum[:, 1, 0:NT], ones[0:NT, :], diag[:], start=True, stop=True).then_inc(route_pe, 1)
                pe.wait_ge(route_dve, route_step(s, COL_SUMMED))
                pe.matmul(psum[:, 2, 0:NT], ones[:], t64[:], start=True, stop=True).then_inc(route_pe, 1)
            pe.wait_ge(route_act, 4 * SINKHORN_ITERS)
            pe.wait_ge(route_dve, MEMBER_STEP)
            for k in range(K):
                last = pe.matmul(psum[0:NT, 0, k:k + 1], member[:, k, :], ones_h[:, 0:1], start=True, stop=True)
            last.then_inc(route_pe, 1)
            pe.wait_ge(route_dve, TILE_SUM_STEP)
            pe.matmul(psum[0:K, 1, 0:1], tile_sum[:], ones_h[0:NT, 0:1], start=True, stop=True).then_inc(route_pe, 1)
            pe.wait_ge(route_dve, TILE_BEFORE_STEP)
            for g in range(K // KB):
                classes = slice(g * KB, (g + 1) * KB)
                place = psum[:, 4 + g, 0:KB * NT]
                pe.matmul(place, before_h[:], member[:, classes, :].rearrange("p k t -> p (k t)"),
                          start=True, stop=False)
                last = pe.matmul(place, ones_h[0:NT, :], tile_before[:, classes, :].rearrange("p k t -> p (k t)"),
                                 start=False, stop=True)
            last.then_inc(route_pe, 1)
            pe.wait_ge(route_dve, BOUNDS_STEP)
            pe.matmul(psum[:, 2, 0:2 * K], ones[0:K, :], bounds_r[:].rearrange("p a k -> p (a k)"),
                      start=True, stop=True).then_inc(route_pe, 1)
            pe.wait_ge(route_dve, PAIRS_STEP)
            for a in range(2):
                last = pe.matmul(psum[0:1, 3, a * P:(a + 1) * P], pairs[:, a:a + 1], ident[:], start=True, stop=True)
            last.then_inc(route_pe, 1)
            pe.wait_ge(route_dve, PAIR_ROW_STEP)

            def project(n, hb, what):
                zt = zTg[:, hb].rearrange("p g t -> p (g t)")
                if what == "g":
                    wait(pe, za_ready, n + 1)
                    wait(pe, th_done, n)
                    pe.matmul(psum[:, 0, :], w_in[:, WG], zt, start=True, stop=True).then_inc(g_ready, 1)
                if what == "k":
                    wait(pe, kg_done, n)
                    pe.matmul(psum[:, 1, :], w_in[:, WK], zt, start=True, stop=True).then_inc(k_ready, 1)
                if what == "q":
                    wait(pe, rq_done, n)
                    pe.matmul(psum[:, 2, :], w_in[:, WQ], zt, start=True, stop=True).then_inc(q_ready, 1)
                if what == "v":
                    wait(pe, kt_saved, n)
                    for t in range(G):
                        last = pe.matmul(psum[:, 3, t * D:(t + 1) * D], zTg[:, hb, t, :], w_in[:, WV],
                                         start=True, stop=True)
                    last.then_inc(v_ready, 1)

            def group(b, hb, last_group):
                n = GB * b + hb
                wait(pe, kp_done, n + 1)
                wait(pe, qp_done, n + 1)
                wait(pe, a_masked, n)
                for c in range(G):
                    last = pe.matmul(psum[:, 4, c * P:(c + 1) * P], kp[:, hb, c, :], qp[:, hb, c, :],
                                     start=True, stop=True)
                last.then_inc(a_ready, 1)
                wait(pe, v_saved, n + 1)
                for c in range(G):
                    last = pe.transpose(psum[:, 3, c * P:(c + 1) * P], kp[:, hb, c, :], ident[:])
                last.then_inc(kt_ready, 1)
                for c, what in enumerate("gkqv"):
                    cb = G * hb + c
                    if not last_group:
                        project(n + 1, 1 - hb, what)
                    if c == 0:
                        wait(pe, kt_saved, n + 1)
                    if cb < C - 1:
                        wait(pe, s_saved, (C - 1) * b + cb)
                        pe.matmul(psum[:, 5, 0:D1], ktok[:, c, :], v1[:, hb, c, :],
                                  start=(cb == 0), stop=True, skip_group_check=True).then_inc(s_ready, 1)
                wait(pe, a_masked, n + 1)
                wait(pe, o_used, n)
                for c in range(G):
                    cb = G * hb + c
                    o = psum[:, 6 + c // 2, (c % 2) * D1:(c % 2 + 1) * D1]
                    last = pe.matmul(o, scores[:, hb, c, :], v1[:, hb, c, :], start=True, stop=(cb == 0))
                    if cb > 0:
                        wait(pe, s_saved, (C - 1) * b + cb)
                        last = pe.matmul(o, qp[:, hb, c, :], state[:, cb, :], start=False, stop=True)
                last.then_inc(o_ready, 1)

            for what in "gkqv":
                project(0, 0, what)

            def batch(b, is_last):
                for hb in range(GB):
                    group(b, hb, is_last and hb == GB - 1)
            loop_and_last(pe, B, batch)

            def turn_row(m, q):
                pe.wait_ge(row_in[q], 16 * (m + 1))
                pe.transpose(psum[:, 6, 0:P], row[:, q, 0:D], ident[:]).then_inc(row_turned, 1)

            def experts_of(i, tiles):
                _, numbers = nc.values_load_multi_w_load_instructions(
                    pair_row[:].rearrange("o t a -> o (t a)")[:, bass.ds(2 * i, 2 * tiles)],
                    engines=[mybir.EngineType.PE], min_val=0, max_val=E - 1, bass_reorder=False,
                    skip_runtime_bounds_check_because="a sum of at most one of pair_of's entries, all below E")
                return numbers

            def up(i, e, j, number):
                if e == 0:
                    wait(pe, xT_ready, i + 1)
                high, low = (w[:, bass.ds(number, 1), :].rearrange("p a f -> p (a f)") for w in (w_high, w_low))
                pe.matmul(psum[:, e, :], xT_high[:, j, :], high, start=True, stop=False)
                pe.matmul(psum[:, e, :], xT_high[:, j, :], low, start=False, stop=False)
                pe.matmul(psum[:, e, :], xT_low[:, j, :], high, start=False, stop=True).then_inc(gu_ready, 1)

            def turn(k, e):
                wait(pe, h_done, k + 1)
                for f in range(FB):
                    last = pe.transpose(psum[:, 2 + e, f * P:(f + 1) * P], h[:, e, f * P:(f + 1) * P], ident[:])
                last.then_inc(hT_ready, 1)

            def down(i, e, j, number):
                wait(pe, hT_saved, 2 * i + e + 1)
                if e == 0:
                    wait(pe, y_saved, i - 1)
                for f in range(FB):
                    weights = w_o[:, bass.ds(number, 1), f, :].rearrange("p a d -> p (a d)")
                    last = pe.matmul(psum[:, 4 + j, 0:D], hT[:, e, f, :], weights,
                                     start=(e == 0 and f == 0), stop=(e == 1 and f == FB - 1))
                last.then_inc(wo_done, 1)

            def four_tiles(m, is_last):
                numbers = experts_of(m * TILES, TILES + 2)
                for k in range(2 * TILES):
                    q, e = k // 2, k % 2
                    i = m * TILES + q
                    if not (is_last and k + 1 >= 2 * TILES):
                        turn(2 * i + e + 1, 1 - e)
                    down(i, e, q % 2, numbers[k])
                    if e == 0 and not (is_last and q >= TILES - 2):
                        turn_row(m + (q + 2) // TILES, (q + 2) % TILES)
                    ahead = k + 3
                    if not (is_last and ahead >= 2 * TILES):
                        up(m * TILES + ahead // 2, ahead % 2, ahead // 2 % 2, numbers[ahead])
            pe.wait_ge(ew_loaded, 48)
            pe.wait_ge(w_split, 2)
            wait(pe, o_used, NG)
            first = experts_of(0, 2)
            turn_row(0, 0)
            wait(pe, xT_ready, 1)
            turn_row(0, 1)
            up(0, 0, 0, first[0])
            up(0, 1, 0, first[1])
            turn(0, 0)
            up(1, 0, 1, first[2])
            loop_and_last(pe, NS // TILES, four_tiles)


_INS = ["L0_attn_x", "L0_attn_qkv_w", "L0_attn_qkv_b", "L0_attn_gate_w", "L0_attn_gate_b", "L0_attn_ln_g",
        "L0_attn_ln_b", "L0_ffn_router_w", "L0_ffn_router_b", "L0_ffn_temperature", "L0_ffn_wg", "L0_ffn_wp",
        "L0_ffn_wo"]


def kernel(**inputs):
    import numpy as np
    import concourse.bacc as bacc
    from concourse.bass_utils import run_bass_kernel_spmd

    nc = bacc.Bacc("TRN2", target_bir_lowering=False, num_devices=1)
    arrays, args = {}, []
    for name in _INS:
        a = np.ascontiguousarray(inputs[name])
        arrays["in_" + name] = a
        args.append(nc.dram_tensor("in_" + name, a.shape, mybir.dt.from_np(a.dtype), kind="ExternalInput").ap())
    shape = arrays["in_L0_attn_x"].shape
    out = nc.dram_tensor("out", shape, F32, kind="ExternalOutput").ap()
    sparse_block_kernel(nc, *args, out)
    r = run_bass_kernel_spmd(nc, [arrays], core_ids=[0])
    return r.results[0]["out"]
```
